# Optimizing a Trainium2 kernel written in Bass

```python
import numpy as np
import jax
import jax.numpy as jnp

def _softmax(x, axis=-1):
    return jax.nn.softmax(x, axis=axis)

def _gelu(x):
    return jax.nn.gelu(x, approximate=True)

def _silu(x):
    return jax.nn.silu(x)

def _sigmoid(x):
    return jax.nn.sigmoid(x)

def _layernorm(x, axis=-1, eps=1e-05):
    m = jnp.mean(x, axis=axis, keepdims=True)
    v = jnp.var(x, axis=axis, keepdims=True)
    return (x - m) / jnp.sqrt(v + eps)

def _scatter_add(tgt, idx, src, axis=0):
    return tgt.at[idx].add(src)

def _segment_sum(src, seg, n):
    return jax.ops.segment_sum(src, seg, n)
kernel_name = 'mk_macaron_d1_jaxref_r8_06f719'

def setup_inputs(seed: int=0):
    np.random.seed(seed)
    _w = jnp.asarray

    def _L0_attn_setup():
        import jax, jax.numpy as jnp
        import numpy as np
        import math
        B, S, DIM = (1, 256, 128)
        H, KVH = (16, 4)
        HD = DIM // H
        KV_DIM = KVH * HD

        def _rms_norm(x):
            eps = jnp.finfo(x.dtype).eps
            return x * jax.lax.rsqrt(jnp.mean(x * x, axis=-1, keepdims=True) + eps)

        def _polar_rotary(seq_len, head_dim, dtype):
            angles = jnp.arange(0, head_dim, 2, dtype=jnp.float32) / head_dim * math.pi
            pos = jnp.arange(seq_len, dtype=jnp.float32)
            radius = 1.0 / (1.0 + pos[:, None] * 0.01)
            ang = pos[:, None] * angles[None, :]
            cos = (radius * jnp.cos(ang)).astype(dtype)
            sin = (radius * jnp.sin(ang)).astype(dtype)
            return (cos[None, None], sin[None, None])

        def _apply_rotary(x, cos, sin):
            half = x.shape[-1] // 2
            x1, x2 = (x[..., :half], x[..., half:])
            return jnp.concatenate([x1 * cos + x2 * sin, x1 * -sin + x2 * cos], axis=-1)

        def _causal_attn(q, k, v, scale, mask):
            s = jnp.einsum('bhqd,bhkd->bhqk', q, k) * scale
            s = jnp.where(mask, s, jnp.finfo(s.dtype).min)
            p = jax.nn.softmax(s, axis=-1)
            return jnp.einsum('bhqk,bhkd->bhqd', p, v)
        key = jax.random.key(seed)
        ks = jax.random.split(key, 8)
        std = 0.02
        return {'x': jax.random.normal(ks[0], (B, S, DIM), jnp.float32), 'Wq': jax.random.normal(ks[1], (DIM, DIM), jnp.float32) * std, 'Wk': jax.random.normal(ks[2], (KV_DIM, DIM), jnp.float32) * std, 'Wv': jax.random.normal(ks[3], (KV_DIM, DIM), jnp.float32) * std, 'Wg': jax.random.normal(ks[4], (KV_DIM, DIM), jnp.float32) * std, 'Wo': jax.random.normal(ks[5], (DIM, DIM), jnp.float32) * std, 'q_gain': jnp.full((H,), 1.0, jnp.float32), 'lambda_param': jnp.full((H,), 0.5, jnp.float32)}
    _L0_attn_in = _L0_attn_setup()

    def _L0_ffn_setup():
        import jax, jax.numpy as jnp
        import numpy as np
        B, S, H = (4, 256, 128)
        D = 256
        E = 8
        K = 2
        key = jax.random.key(seed)
        ks = jax.random.split(key, 8)
        w = lambda k, shape: jax.random.normal(k, shape, jnp.float32) * 0.02
        return {'hidden_states': jax.random.normal(ks[0], (B, S, H), jnp.float32), 'gate_w': w(ks[1], (H, E)), 'w_gate': w(ks[2], (E, H, D)), 'w_up': w(ks[3], (E, H, D)), 'w_down': w(ks[4], (E, D, H)), 'ws_gate': w(ks[5], (H, D)), 'ws_up': w(ks[6], (H, D)), 'ws_down': w(ks[7], (D, H))}
    _L0_ffn_in = _L0_ffn_setup()
    _d = {'L0_attn_x': _L0_attn_in['x'], 'L0_attn_Wq': _L0_attn_in['Wq'], 'L0_attn_Wk': _L0_attn_in['Wk'], 'L0_attn_Wv': _L0_attn_in['Wv'], 'L0_attn_Wg': _L0_attn_in['Wg'], 'L0_attn_Wo': _L0_attn_in['Wo'], 'L0_attn_q_gain': _L0_attn_in['q_gain'], 'L0_attn_lambda_param': _L0_attn_in['lambda_param'], 'L0_ffn_gate_w': _L0_ffn_in['gate_w'], 'L0_ffn_w_gate': _L0_ffn_in['w_gate'], 'L0_ffn_w_up': _L0_ffn_in['w_up'], 'L0_ffn_w_down': _L0_ffn_in['w_down'], 'L0_ffn_ws_gate': _L0_ffn_in['ws_gate'], 'L0_ffn_ws_up': _L0_ffn_in['ws_up'], 'L0_ffn_ws_down': _L0_ffn_in['ws_down']}
    _x0 = _d['L0_attn_x']
    _d['L0_attn_x'] = jax.random.normal(jax.random.fold_in(jax.random.key(seed), 1), (16, 256, 128), dtype=_x0.dtype)
    del _x0
    return _d

def reference(L0_attn_x, L0_attn_Wq, L0_attn_Wk, L0_attn_Wv, L0_attn_Wg, L0_attn_Wo, L0_attn_q_gain, L0_attn_lambda_param, L0_ffn_gate_w, L0_ffn_w_gate, L0_ffn_w_up, L0_ffn_w_down, L0_ffn_ws_gate, L0_ffn_ws_up, L0_ffn_ws_down):

    def _L0_attn_ref(x, Wq, Wk, Wv, Wg, Wo, q_gain, lambda_param):
        import jax, jax.numpy as jnp
        import numpy as np
        import math
        B, S, DIM = (1, 256, 128)
        H, KVH = (16, 4)
        HD = DIM // H
        KV_DIM = KVH * HD

        def _rms_norm(x):
            eps = jnp.finfo(x.dtype).eps
            return x * jax.lax.rsqrt(jnp.mean(x * x, axis=-1, keepdims=True) + eps)

        def _polar_rotary(seq_len, head_dim, dtype):
            angles = jnp.arange(0, head_dim, 2, dtype=jnp.float32) / head_dim * math.pi
            pos = jnp.arange(seq_len, dtype=jnp.float32)
            radius = 1.0 / (1.0 + pos[:, None] * 0.01)
            ang = pos[:, None] * angles[None, :]
            cos = (radius * jnp.cos(ang)).astype(dtype)
            sin = (radius * jnp.sin(ang)).astype(dtype)
            return (cos[None, None], sin[None, None])

        def _apply_rotary(x, cos, sin):
            half = x.shape[-1] // 2
            x1, x2 = (x[..., :half], x[..., half:])
            return jnp.concatenate([x1 * cos + x2 * sin, x1 * -sin + x2 * cos], axis=-1)

        def _causal_attn(q, k, v, scale, mask):
            s = jnp.einsum('bhqd,bhkd->bhqk', q, k) * scale
            s = jnp.where(mask, s, jnp.finfo(s.dtype).min)
            p = jax.nn.softmax(s, axis=-1)
            return jnp.einsum('bhqk,bhkd->bhqd', p, v)
        bsz, seqlen, dim = x.shape
        q = (x @ Wq.T).reshape(bsz, seqlen, H, HD).transpose(0, 2, 1, 3)
        k = (x @ Wk.T).reshape(bsz, seqlen, KVH, HD).transpose(0, 2, 1, 3)
        v = (x @ Wv.T).reshape(bsz, seqlen, KVH, HD).transpose(0, 2, 1, 3)
        v_g = jax.nn.sigmoid((x @ Wg.T).reshape(bsz, seqlen, KVH, HD).transpose(0, 2, 1, 3))
        v = v * v_g
        q = _rms_norm(q)
        k = _rms_norm(k)
        cos, sin = _polar_rotary(seqlen, HD, q.dtype)
        q = _apply_rotary(q, cos, sin)
        k = _apply_rotary(k, cos, sin)
        q = q * q_gain.astype(q.dtype)[None, :, None, None]
        rep = H // KVH
        k = jnp.repeat(k, rep, axis=1)
        v = jnp.repeat(v, rep, axis=1)
        half = HD // 2
        q1, q2 = (q[..., :half], q[..., half:])
        k1, k2 = (k[..., :half], k[..., half:])
        v1, v2 = (v[..., :half], v[..., half:])
        scale = 1.0 / math.sqrt(half)
        mask = jnp.tril(jnp.ones((seqlen, seqlen), dtype=bool))[None, None]
        a1 = _causal_attn(q1, k1, v1, scale, mask)
        a2 = _causal_attn(q2, k2, v2, scale, mask)
        lp = lambda_param.astype(q.dtype)[None, :, None, None]
        y = jnp.concatenate([a1 - lp * a2, a1 + lp * a2], axis=-1)
        y = y.transpose(0, 2, 1, 3).reshape(bsz, seqlen, dim)
        return y @ Wo.T

    def _L0_ffn_ref(hidden_states, gate_w, w_gate, w_up, w_down, ws_gate, ws_up, ws_down):
        import jax, jax.numpy as jnp
        import numpy as np
        B, S, H = (4, 256, 128)
        D = 256
        E = 8
        K = 2
        b, s, h = hidden_states.shape
        x = hidden_states.reshape(-1, h)
        scores = jax.nn.softmax(x @ gate_w, axis=-1)
        topk_w, topk_idx = jax.lax.top_k(scores, K)
        topk_w = topk_w / (jnp.sum(topk_w, axis=-1, keepdims=True) + 1e-20)
        onehot = jax.nn.one_hot(topk_idx, E, dtype=x.dtype)
        w_per_expert = jnp.einsum('nke,nk->ne', onehot, topk_w)
        y = jnp.zeros_like(x)
        for e in range(E):
            hid = jax.nn.silu(x @ w_gate[e]) * (x @ w_up[e])
            y = y + w_per_expert[:, e:e + 1] * (hid @ w_down[e])
        shared = jax.nn.silu(x @ ws_gate) * (x @ ws_up) @ ws_down
        return (y + shared).reshape(b, s, h)
    x = L0_attn_x
    x = x + 0.5 * _L0_ffn_ref(_layernorm(x, axis=-1), L0_ffn_gate_w, L0_ffn_w_gate, L0_ffn_w_up, L0_ffn_w_down, L0_ffn_ws_gate, L0_ffn_ws_up, L0_ffn_ws_down)
    x = x + _L0_attn_ref(_layernorm(x, axis=-1), L0_attn_Wq, L0_attn_Wk, L0_attn_Wv, L0_attn_Wg, L0_attn_Wo, L0_attn_q_gain, L0_attn_lambda_param)
    x = x + 0.5 * _L0_ffn_ref(_layernorm(x, axis=-1), L0_ffn_gate_w, L0_ffn_w_gate, L0_ffn_w_up, L0_ffn_w_down, L0_ffn_ws_gate, L0_ffn_ws_up, L0_ffn_ws_down)
    return x

_drawn_inputs = setup_inputs


def setup_inputs(seed=0):
    import zlib

    import numpy as np

    out = dict(_drawn_inputs(seed))
    spreads = {'L0_attn_q_gain': (1.0, 0.6), 'L0_attn_lambda_param': (0.5, 0.6)}
    factors = {'L0_attn_Wq': 8.0,
     'L0_attn_Wk': 8.0,
     'L0_attn_Wv': 8.0,
     'L0_attn_Wg': 8.0,
     'L0_attn_Wo': 8.0,
     'L0_ffn_gate_w': 8.0,
     'L0_ffn_w_gate': 8.0,
     'L0_ffn_w_up': 8.0,
     'L0_ffn_w_down': 8.0,
     'L0_ffn_ws_gate': 6.901,
     'L0_ffn_ws_up': 6.814,
     'L0_ffn_ws_down': 6.823}
    for name, (base, spread) in spreads.items():
        noise = np.random.default_rng([zlib.crc32(name.encode()), seed]).standard_normal(out[name].shape)
        drawn = base * np.exp(spread * noise) if base else spread * noise
        out[name] = jnp.asarray(drawn.astype(out[name].dtype))
    for name, factor in factors.items():
        out[name] = (out[name] * factor).astype(out[name].dtype)
    return out
```

```python
from contextlib import ExitStack

import concourse.bass as bass
from concourse import mybir

F32 = mybir.dt.float32
F32R = mybir.dt.float32r
BF16 = mybir.dt.bfloat16
ALU = mybir.AluOpType
ACT = mybir.ActivationFunctionType
AX = mybir.AxisListType

P = 128
BATCH, SEQ, DIM = 16, 256, 128
TOKT = BATCH * SEQ // P
TILE = 512
SUB = TILE // P
NT = BATCH * SEQ // TILE
E, HID = 8, 256
NCH = (E + 1) * 2
LEAD = 4
HEADS, KVH, HD = 16, 4, 8
HALF = HD // 2
REP = HEADS // KVH
QKV = DIM + 3 * KVH * HD
NH = HEADS + KVH
GRP = 32
LN_EPS = 1e-5
RMS_EPS = 1.1920928955078125e-07
NEG = -1.0e30
UNITS = 24
T_LAG = 4
SLOTS = UNITS + T_LAG


class Links:

    def __init__(self, engine, sem):
        self.engine, self.sem, self.base, self.n = engine, sem, 0, 0

    def done(self, ins, apart=None):
        self.n += 1
        ins.then_inc(self.sem, 1)
        if apart:
            wait_apart(self.engine, self.sem, self.base + self.n, apart)
        else:
            self.engine.wait_ge(self.sem, self.base + self.n)

    def enter(self, i, per):
        self.start, self.per = self.base + self.n, per
        self.base, self.n = self.start + i * per, 0

    def leave(self, times):
        assert self.n == self.per, f"{self.n} steps in the body, not {self.per}"
        self.base, self.n = self.start + times * self.per, 0


def wait_apart(engine, sem, value, passed):
    engine.wait_ge(sem, value)
    engine.sem_inc(passed, 1)


def macaron(nc, x_in, w_gate, w_up, w_down, ws_gate, ws_up, ws_down, gate_w, wqkv, wo, q_gain, lam, rot, out):
    ctx = ExitStack()
    with ctx:
        def sb(name, shape, dt=F32):
            return ctx.enter_context(nc.sbuf_tensor(name, shape, dt))

        def sem(name):
            return ctx.enter_context(nc.semaphore(name))

        bank = [ctx.enter_context(nc.psum_tensor(f"bank{i}", [P, 512], F32)) for i in range(8)]
        g_ps, u_ps, y_ps, xw_ps, prep_ps, fin_ps = bank[0:2], bank[2:4], bank[4], bank[5], bank[6], bank[7]
        s_ps, t_ps, o_ps, a_ps, qT_ps, e_ps = bank[0:2], bank[2:4], bank[4], bank[5], bank[6], bank[7]

        x_sb = sb("x_sb", [P, TOKT, DIM])
        w_raw = sb("w_raw", [P, E + 1, 3, HID])
        w_hi = sb("w_hi", [P, E + 1, 3, HID], F32R)
        w_lo = sb("w_lo", [P, E + 1, 3, HID], F32R)
        pr = w_raw[:].rearrange("p e j d -> p (e j d)")[:, 0:6144].rearrange("p (a j n) -> p a j n", a=2, j=6)
        arena = sb("arena", [P, 7168], F32R)

        def cut(at, *dims):
            size = 1
            for d in dims:
                size *= d
            names_ = "abcd"[:len(dims)]
            flat = arena[:, at:at + size]
            return flat.rearrange(f"p ({' '.join(names_)}) -> p {' '.join(names_)}", **dict(zip(names_, dims)))

        gw_raw, gw_hi, gw_lo = sb("gw_raw", [P, E]), sb("gw_hi", [P, E], F32R), sb("gw_lo", [P, E], F32R)
        wa_raw = sb("wa_raw", [P, QKV + DIM])
        wa_hi, wa_lo = sb("wa_hi", [P, QKV + DIM], F32R), sb("wa_lo", [P, QKV + DIM], F32R)
        ident = sb("ident", [P, P])
        ident_b = sb("ident_b", [P, P], BF16)
        mask_b = sb("mask_b", [P, KVH, P], BF16)
        minus_half = sb("minus_half", [P, 2 * NH])
        before = sb("before", [P, E, E])
        after = sb("after", [P, E, E])

        st = sb("st", [P, SUB, 6])
        mv = sb("mv", [P, SUB, 2])
        rstd = sb("rstd", [P, SUB])
        xn = sb("xn", [P, 2, SUB, DIM])
        x_hi, x_lo = cut(0, 2, TILE), cut(1024, 2, TILE)
        lmax = sb("lmax", [P, SUB])
        lsub = sb("lsub", [P, SUB, E])
        prob = sb("prob", [P, SUB, E])
        cmp_ge, cmp_gt = sb("cmp_ge", [P, SUB, E, E]), sb("cmp_gt", [P, SUB, E, E])
        rank, chosen = sb("rank", [P, SUB, E]), sb("chosen", [P, SUB, E])
        total, top2, rtop = sb("total", [P, SUB]), sb("top2", [P, SUB]), sb("rtop", [P, SUB])
        w_tok = sb("w_tok", [P, 2, SUB, E])
        xw = sb("xw", [P, 2, SUB, DIM])
        xw_hi, xw_lo = cut(2048, 2, TILE), cut(3072, 2, TILE)
        act_g = sb("act_g", [P, 2, TILE])
        hid = sb("hid", [P, 2, TILE])
        h_hi, h_lo = cut(4096, 3, TILE), cut(5632, 3, TILE)
        y_sb = sb("y_sb", [P, TILE])

        rot_sb = sb("rot_sb", [P, 2, 2, HALF])
        cc = sb("cc", [P, 2, HD])
        ss = sb("ss", [P, 2, HD])
        gain_in = sb("gain_in", [P, HEADS])
        lam_in = sb("lam_in", [P, HEADS])
        gain = sb("gain", [P, 2, NH])
        lam_x = sb("lam_x", [P, REP, 2, KVH, HALF])
        ast, amv, arstd = sb("ast", [P, 2, 6]), sb("amv", [P, 2, 2]), sb("arstd", [P, 2])
        xa = sb("xa", [P, 2, DIM])
        xa_hi, xa_lo = sb("xa_hi", [P, 2 * P], F32R), sb("xa_lo", [P, 2 * P], F32R)
        qkv = sb("qkv", [P, 2, QKV])
        eg = sb("eg", [P, 2, KVH * HD])
        sq = sb("sq", [P, 2, NH, HD])
        ms = sb("ms", [P, 2, NH])
        ma, r0, lnm = sb("ma", [P, 2, NH]), sb("r0", [P, 2, NH]), sb("lnm", [P, 2, NH])
        rq = sb("rq", [P, 2, NH])
        eps_col = sb("eps_col", [P, 1])
        th, th1 = sb("th", [P, SUB, E]), sb("th1", [P, SUB, E])
        qn = sb("qn", [P, 2, NH, HD])
        ra, rb = sb("ra", [P, 2, NH, HD]), sb("rb", [P, 2, NH, HD])
        qs = sb("qs", [P, 2, 2, 2, REP, KVH, GRP])
        ks = sb("ks", [P, 2, 2, KVH, GRP])
        q1 = cut(0, 2, 2, REP, SEQ)
        q2 = cut(4096, 2, REP, SEQ)
        kb = sb("kb", [P, 2, 2, KVH, SEQ], F32R)
        v1 = sb("v1", [P, 2, 2, 2, KVH, GRP])
        mx = sb("mx", [P, 3, 2, REP, KVH])
        o_sb = act_g
        rden = sb("rden", [P, 16])
        an = sb("an", [P, 2, 2, 16, HALF])
        ya = sb("ya", [P, 2, HEADS, HD])
        lt = sb("lt", [P, P])
        ya_hi, ya_lo = sb("ya_hi", [P, 2 * P], F32R), sb("ya_lo", [P, 2 * P], F32R)

        names = """x_loaded w_loaded small_loaded x_stored consts w_hi_done w_lo_done
            stats_done rstd_done xn_done xnT_done xhi_done xlo_done logits_done lsub_done tanh_done
            wtok_done xw_done xwT_done xwhi_done xwlo_done g_done u_done silu_done hid_done hhi_done
            hlo_done down_done y_done yT_done xnew_done dve_self pool_self
            a_stats a_rstd a_xn a_xnT a_xhi a_xlo a_proj a_qkv a_eg a_ms a_r0 a_rq act_self a_v a_stack a_kT a_kb
            a_q1T a_q1 s_done max_done m_done q2T_done q2_done t_done exp_done sel_done pv_done
            o_done oT_done an_done ya_done yaT_done yahi_done yalo_done wo_done att_done passed""".split()
        S = {n: sem(n) for n in names}
        (x_loaded, w_loaded, small_loaded, x_stored, consts, w_hi_done, w_lo_done,
         stats_done, rstd_done, xn_done, xnT_done, xhi_done, xlo_done, logits_done, lsub_done, tanh_done,
         wtok_done, xw_done, xwT_done, xwhi_done, xwlo_done, g_done, u_done, silu_done, hid_done, hhi_done,
         hlo_done, down_done, y_done, yT_done, xnew_done, dve_self, pool_self,
         a_stats, a_rstd, a_xn, a_xnT, a_xhi, a_xlo, a_proj, a_qkv, a_eg, a_ms, a_r0, a_rq, act_self, a_v, a_stack, a_kT, a_kb,
         a_q1T, a_q1, s_done, max_done, m_done, q2T_done, q2_done, t_done, exp_done, sel_done, pv_done,
         o_done, oT_done, an_done, ya_done, yaT_done, yahi_done, yalo_done, wo_done, att_done, passed) = [S[n] for n in names]

        ORDER = [E] + list(range(E))
        x_tok = x_in.rearrange("b (j p) d -> p (b j) d", p=P)
        out_tok = out.rearrange("b (j p) d -> p (b j) d", p=P)
        N_CONST = 10
        N_SMALL = 6

        block = ctx.enter_context(nc.Block())

        def ffn_stage(stage, step, prep, finish, tail, links=None, per=0):
            t0 = stage * NT

            def tile(t, par, last):
                for n in range(LEAD, NCH):
                    step(t, n, par, False, last)
                    if not last:
                        prep(t + 1, 1 - par, n)
                if not last:
                    for n in range(LEAD):
                        step(t + 1, n, 1 - par, False, False)
                    finish(t, par, last)
                else:
                    tail(t, par)
                    finish(t, par, last)

            for n in range(LEAD, NCH):
                prep(t0, 0, n)
            for n in range(LEAD):
                step(t0, n, 0, True, False)
            with (links[0].engine if links else engine_of[0]).Fori(0, NT // 2 - 1) as i:
                if links:
                    for li in links:
                        li.enter(i, per)
                tile(t0 + 2 * i, 0, False)
                tile(t0 + 2 * i + 1, 1, False)
            if links:
                for li in links:
                    li.leave(NT // 2 - 1)
            tile(t0 + NT - 2, 0, False)
            tile(t0 + NT - 1, 1, True)

        engine_of = [None]

        def attention(piece, per=0, links=None):
            def step(b, p, scores=True, late=True, tail=True, ahead=True):
                for slot in range(SLOTS):
                    piece(b, p, slot, scores, late, tail, ahead)

            def first():
                for slot in range(SLOTS):
                    piece(-1, 1, slot, False, False, False, True)
            first()
            step(0, 0, late=False, tail=False)
            step(1, 1, tail=False)
            loops = (BATCH - 4) // 2
            with (links[0].engine if links else engine_of[0]).Fori(0, loops) as i:
                if links:
                    for li in links:
                        li.enter(i, per)
                step(2 + 2 * i, 0)
                step(3 + 2 * i, 1)
            if links:
                for li in links:
                    li.leave(loops)
            step(BATCH - 2, 0)
            step(BATCH - 1, 1, ahead=False)
            step(BATCH, 0, scores=False, ahead=False)
            step(BATCH + 1, 1, scores=False, late=False, ahead=False)

        COMBOS = [(0, 0, True), (1, 0, False), (1, 1, True)]
        S_UNITS = [(half, rep, c) for half in range(2) for rep in range(REP) for c in range(3)]

        S_SLOT = {slot: n for n, slot in enumerate(x for x in range(SLOTS) if x not in (8, 15, 17, 19))}

        @block.sync
        def _(sp):
            with sp.Fori(0, NT) as t:
                sp.dma_start(x_sb[:, bass.ds(t * SUB, SUB), :], x_tok[:, bass.ds(t * SUB, SUB), :]).then_inc(x_loaded, 16)
                wait_apart(sp, x_loaded, t * 16 + 16, passed)
            with sp.Fori(0, NT) as t:
                sp.wait_ge(xnew_done, t + NT + 1)
                sp.dma_start(out_tok[:, bass.ds(t * SUB, SUB), :], x_sb[:, bass.ds(t * SUB, SUB), :]).then_inc(x_stored, 16)
            sp.wait_ge(x_stored, 16 * NT)

        @block.gpsimd
        def _(pool):
            self_ = Links(pool, pool_self)
            pool.dma_start(gw_raw[:], gate_w).then_inc(small_loaded, 16)
            pool.dma_start(wa_raw[:, 0:QKV], wqkv).then_inc(small_loaded, 16)
            pool.dma_start(wa_raw[:, QKV:], wo).then_inc(small_loaded, 16)
            pool.dma_start(rot_sb[:], rot.rearrange("(j p) a d -> p j a d", p=P)).then_inc(small_loaded, 16)
            pool.dma_start(gain_in[:], q_gain.rearrange("(a h) -> a h", a=1).broadcast_to((P, HEADS))).then_inc(small_loaded, 16)
            pool.dma_start(lam_in[:], lam.rearrange("(a h) -> a h", a=1).broadcast_to((P, HEADS))).then_inc(small_loaded, 16)
            g = nc.gpsimd
            g.memset(minus_half[:], -0.5).then_inc(consts, 1)
            self_.done(g.memset(ident[:], 0.0))
            self_.done(g.memset(ident_b[:], 0.0))
            self_.done(g.memset(mask_b[:], 0.0))
            self_.done(g.memset(before[:], 1.0))
            self_.done(g.memset(after[:], 1.0))
            g.affine_select(out=ident[:], in_=ident[:], compare_op=ALU.not_equal, fill=1.0, base=0,
                            pattern=[[-1, P]], channel_multiplier=1).then_inc(consts, 1)
            g.affine_select(out=ident_b[:], in_=ident_b[:], compare_op=ALU.not_equal, fill=1.0, base=0,
                            pattern=[[-1, P]], channel_multiplier=1).then_inc(consts, 1)
            g.affine_select(out=mask_b[:], in_=mask_b[:], compare_op=ALU.is_ge, fill=NEG, base=0,
                            pattern=[[0, KVH], [-1, P]], channel_multiplier=1).then_inc(consts, 1)
            g.affine_select(out=before[:], in_=before[:], compare_op=ALU.is_gt, fill=0.0, base=0,
                            pattern=[[1, E], [-1, E]], channel_multiplier=0).then_inc(consts, 1)
            g.affine_select(out=after[:], in_=after[:], compare_op=ALU.is_gt, fill=0.0, base=0,
                            pattern=[[-1, E], [1, E]], channel_multiplier=0).then_inc(consts, 1)
            self_.done(g.memset(qs[:], 0.0))
            self_.done(g.memset(ks[:], 0.0))
            self_.done(g.memset(v1[:], 0.0))
            g.memset(ks[:, :, :, :, 12:14], 1.0).then_inc(consts, 1)
            g.memset(v1[:, :, :, :, :, HALF:HALF + 1], 1.0).then_inc(consts, 1)
            g.memset(kb[:].bitcast(F32), 0.0).then_inc(consts, 1)
            g.memset(eps_col[:], RMS_EPS)
            g.memset(gain[:], 1.0).then_inc(consts, 1)

            def power(t):
                wait_apart(pool, stats_done, t + 1, passed)
                self_.done(g.tensor_scalar(rstd[:], mv[:, :, 1], LN_EPS, 1.0, ALU.add, ALU.mult))
                g.tensor_tensor(rstd[:], rstd[:], minus_half[:, 0:SUB], ALU.pow).then_inc(rstd_done, 1)

            def scale(t, par, k):
                pool.wait_ge(wtok_done, t + 1)
                wait_apart(pool, xwT_done, t * E + k - 2, passed)
                for j in range(SUB):
                    ins = g.tensor_scalar(xw[:, k % 2, j, :], xn[:, par, j, :], w_tok[:, par, j, k - 1:k], 1.0,
                                          ALU.mult, ALU.mult)
                ins.then_inc(xw_done, 1)

            def scale_first(t, par, k):
                wait_apart(pool, wtok_done, t + 1, passed)
                for j in range(SUB):
                    ins = g.tensor_scalar(xw[:, k % 2, j, :], xn[:, par, j, :], w_tok[:, par, j, k - 1:k], 1.0,
                                          ALU.mult, ALU.mult)
                ins.then_inc(xw_done, 1)

            def step(t, n, par, first, last):
                if n % 2 == 0 and 3 <= n // 2 + 2 <= E:
                    scale(t, par, n // 2 + 2)

            def prep_at(stage):
                def prep(t, par, n):
                    if n == 4:
                        power(t)
                    if n in (14, 16):
                        (scale_first if isinstance(t, int) and t == 0 else scale)(t, par, (n - 12) // 2)
                return prep

            def nothing(*a):
                pass

            def piece(b, p, slot, scores, late, tail, ahead):
                if ahead and slot == 2:
                    wait_apart(pool, a_stats, b + 2, passed)
                    self_.done(g.tensor_scalar(arstd[:], amv[:, :, 1], LN_EPS, 1.0, ALU.add, ALU.mult))
                    g.tensor_tensor(arstd[:], arstd[:], minus_half[:, 0:2], ALU.pow).then_inc(a_rstd, 1)
                if ahead and slot == 11:
                    wait_apart(pool, a_r0, b + 2, passed)
                    self_.done(g.tensor_scalar(ma[:], ms[:], 1.0 / HD, RMS_EPS, ALU.mult, ALU.add))
                    self_.done(g.tensor_tensor(ma[:], ma[:], r0[:], ALU.mult))
                    self_.done(g.tensor_tensor(ma[:], ma[:], r0[:], ALU.mult), apart=passed)
                    self_.done(g.tensor_scalar(ma[:], ma[:], -0.5, 1.5, ALU.mult, ALU.add))
                    self_.done(g.tensor_tensor(ma[:], ma[:], r0[:], ALU.mult))
                    g.tensor_tensor(rq[:], ma[:], gain[:], ALU.mult).then_inc(a_rq, 1)
                u = slot - T_LAG
                if late and u >= 0:
                    hp, j = u // 6, u % 6
                    wait_apart(pool, exp_done, (b - 1) * UNITS + u + 1, passed)
                    if j < 4:
                        v = pr[:, hp % 2, j, :].rearrange("p (i q) -> p i q", i=2)[:, :, 0:P]
                        pat = [[0, 2], [1, P]]
                    else:
                        v = pr[:, hp % 2, j, :].rearrange("p (i q) -> p i q", i=4)
                        pat = [[0, 4], [1, P]]
                    g.affine_select(out=v, in_=v, compare_op=ALU.is_ge, fill=0.0, base=0,
                                    pattern=pat, channel_multiplier=-1).then_inc(sel_done, 1)

            engine_of[0] = pool
            pool.wait_ge(small_loaded, 16 * N_SMALL)
            ffn_stage(0, step, prep_at(0), nothing, nothing, [self_], 2)
            pool.wait_ge(consts, N_CONST + 2)
            attention(piece, 2 * 6, [self_])
            ffn_stage(1, step, prep_at(1), nothing, nothing, [self_], 2)

        @block.scalar
        def _(act):
            s = nc.scalar
            self_ = Links(act, act_self)
            engine_of[0] = act
            for n, e in enumerate(ORDER):
                parts = (ws_gate, ws_up) if e == E else (w_gate[e], w_up[e])
                down = ws_down if e == E else w_down[e]
                for j, part in enumerate(parts):
                    act.dma_start(w_raw[:, e, j, :], part).then_inc(w_loaded, 16)
                act.dma_start(w_raw[:, e, 2, :].rearrange("p (c h) -> p c h", c=2),
                              down.rearrange("(c p) h -> p c h", p=P)).then_inc(w_loaded, 16)
            act.wait_ge(small_loaded, 16 * N_SMALL)
            s.copy(gw_hi[:], gw_raw[:]).then_inc(w_hi_done, 1)
            s.copy(wa_hi[:], wa_raw[:]).then_inc(w_hi_done, 1)
            act.wait_ge(w_loaded, 16 * 3 * (E + 1))
            for e in ORDER:
                s.copy(w_hi[:, e], w_raw[:, e]).then_inc(w_hi_done, 1)

            def hi(m):
                pass

            def step(t, n, par, first, last):
                c = t * NCH + n
                act.wait_ge(g_done, c + 1)
                if not (isinstance(t, int) and t == 0 and n < 2):
                    act.wait_ge(hid_done, c - 1)
                s.activation(act_g[:, n % 2, :], g_ps[n % 2][:], ACT.Silu).then_inc(silu_done, 1)
                if not (first and n == 0):
                    top(t, n - 1)
                if n % 2 == 0 and n // 2 + 1 <= E:
                    k = n // 2 + 1
                    act.wait_ge(xwT_done, t * E + k)
                    if not (isinstance(t, int) and t == 0 and k < 3):
                        act.wait_ge(u_done, c - 2 if k > 2 else c - 1)
                    s.copy(xw_hi[:, k % 2, :], xw_ps[:]).then_inc(xwhi_done, 1)
                if n == 1 and not first:
                    output(t - 1)

            def top(t, n):
                m = t * NCH + n
                act.wait_ge(hid_done, m + 1)
                if not (isinstance(t, int) and t == 0 and n < 3):
                    act.wait_ge(down_done, m - 2)
                s.copy(h_hi[:, n % 3, :], hid[:, n % 2, :]).then_inc(hhi_done, 1)

            def output(t):
                act.wait_ge(down_done, (t + 1) * NCH)
                s.activation(y_sb[:], y_ps[:], ACT.Copy, scale=0.5).then_inc(y_done, 1)

            def prep(t, par, n):
                if n == 7:
                    act.wait_ge(xnT_done, t + 1)
                    s.copy(x_hi[:, par, :], prep_ps[:]).then_inc(xhi_done, 1)
                if n == 10:
                    act.wait_ge(lsub_done, t + 1)
                    s.activation(th[:], lsub[:], ACT.Tanh, scale=0.5).then_inc(tanh_done, 1)

            def tail(t, par):
                top(t, NCH - 1)
                output(t)

            def nothing(*a):
                pass

            def piece(b, p, slot, scores, late, tail, ahead):
                if late and slot in (3, 5, 7, 9):
                    hp = (slot - 3) // 2
                    act.wait_ge(q2T_done, (b - 1) * 4 + hp + 1)
                    s.copy(q2[:, hp // 2, 2 * (hp % 2):2 * (hp % 2) + 2, :],
                           qT_ps[:].rearrange("p (i q) -> p i q", i=2)).then_inc(q2_done, 1)
                if ahead and slot == 4:
                    act.wait_ge(a_xnT, b + 2)
                    s.copy(xa_hi[:], a_ps[:, 0:2 * P]).then_inc(a_xhi, 1)
                if ahead and slot == 8:
                    act.wait_ge(a_proj, b + 2)
                    if not (isinstance(b, int) and b == -1):
                        act.wait_ge(a_stack, 2 * b + 2)
                        act.wait_ge(a_v, b + 1)
                    pj = a_ps[:, 0:2 * QKV].rearrange("p (j c) -> p j c", j=2)
                    s.copy(qkv[:], pj).then_inc(a_qkv, 1)
                    s.activation(eg[:], pj[:, :, QKV - KVH * HD:QKV], ACT.Exp, scale=-1.0).then_inc(a_eg, 1)
                if ahead and slot == 10:
                    act.wait_ge(a_ms, b + 2)
                    self_.done(s.activation(lnm[:], ms[:], ACT.Ln, bias=eps_col[:], scale=1.0 / HD))
                    s.activation(r0[:], lnm[:], ACT.Exp, scale=-0.5).then_inc(a_r0, 1)
                if ahead and slot == 21:
                    place_keys(b + 1, 1 - p, 0)
                if scores and slot == 0:
                    place_keys(b, p, 1)
                if ahead and slot in (20, 22, 24, 26):
                    hp = (slot - 20) // 2
                    act.wait_ge(a_q1T, (b + 1) * 4 + hp + 1)
                    s.copy(q1[:, 1 - p, hp // 2, 2 * (hp % 2):2 * (hp % 2) + 2, :],
                           qT_ps[:].rearrange("p (i q) -> p i q", i=2)).then_inc(a_q1, 1)
                u = slot - T_LAG
                if late and u >= 0:
                    hp = u // 6
                    act.wait_ge(t_done, (b - 1) * UNITS + u + 1)
                    if u % 6 == 0 and not (isinstance(b, int) and b == 1 and hp < 2):
                        act.wait_ge(pv_done, (b - 1) * 4 + hp - 1)
                    s.activation(pr[:, hp % 2, u % 6, :], t_ps[u % 2][:], ACT.Exp, scale=float(HALF) ** -0.5)\
                        .then_inc(exp_done, 1)
                if late and slot in (14, 20, 26):
                    outputs((b - 1) * 4 + (slot - 14) // 6, (slot - 14) // 6, isinstance(b, int) and b == 1)
                if tail and slot == 4:
                    outputs((b - 2) * 4 + 3, 3, False)
                if tail and slot == 10:
                    act.wait_ge(yaT_done, b - 1)
                    s.copy(ya_hi[:], e_ps[:, 0:2 * P]).then_inc(yahi_done, 1)

            def place_keys(b, p, half):
                act.wait_ge(a_kT, 2 * b + half + 1)
                if not (isinstance(b, int) and b < 2):
                    act.wait_ge(t_done, (b - 2) * UNITS + (half + 1) * UNITS // 2)
                for r in range(KVH):
                    rows = slice(GRP * r, GRP * r + GRP)
                    ins = s.copy(kb[rows, p, half, r, :], a_ps[rows, half * 256:half * 256 + 256])
                ins.then_inc(a_kb, 1)

            def outputs(count, hp, fresh):
                act.wait_ge(pv_done, count + 1)
                if not (fresh and hp < 2):
                    act.wait_ge(oT_done, count - 1)
                s.copy(o_sb[:, hp % 2, :], o_ps[:]).then_inc(o_done, 1)

            ffn_stage(0, step, prep, nothing, tail)
            act.wait_ge(consts, N_CONST)
            act.preload_act_table_set("natural_log_exp_and_others")
            attention(piece, 2, [self_])
            ffn_stage(1, step, prep, nothing, tail)

        @block.vector
        def _(dve):
            v = nc.vector
            engine_of[0] = dve
            self_ = Links(dve, dve_self)
            dve.wait_ge(w_hi_done, 1)
            v.tensor_tensor(gw_lo[:], gw_raw[:], gw_hi[:].bitcast(F32), ALU.subtract).then_inc(w_lo_done, 1)
            dve.wait_ge(w_hi_done, 2)
            v.tensor_tensor(wa_lo[:], wa_raw[:], wa_hi[:].bitcast(F32), ALU.subtract).then_inc(w_lo_done, 1)
            v.tensor_copy(cc[:, :, 0:HALF], rot_sb[:, :, 0, :])
            v.tensor_copy(cc[:, :, HALF:HD], rot_sb[:, :, 0, :])
            v.tensor_copy(ss[:, :, 0:HALF], rot_sb[:, :, 1, :])
            v.tensor_scalar(ss[:, :, HALF:HD], rot_sb[:, :, 1, :], -1.0, None, ALU.mult)
            dve.wait_ge(consts, N_CONST)
            for j in range(2):
                v.tensor_copy(gain[:, j, 0:HEADS], gain_in[:]).then_inc(consts, 1)
            for rep in range(REP):
                for j in range(2):
                    ins = v.tensor_copy(lam_x[:, rep, j, :, :],
                                        lam_in[:].rearrange("p (r i) -> p r i", i=REP)[:, :, rep:rep + 1]
                                        .broadcast_to((P, KVH, HALF)))
            self_.done(ins)
            for n, e in enumerate(ORDER):
                dve.wait_ge(w_hi_done, n + 3)
                v.tensor_tensor(w_lo[:, e], w_raw[:, e], w_hi[:, e].bitcast(F32), ALU.subtract).then_inc(w_lo_done, 1)
            def step(t, n, par, first, last):
                c = t * NCH + n
                dve.wait_ge(silu_done, c + 1)
                dve.wait_ge(u_done, c + 1)
                if not (isinstance(t, int) and t == 0 and n < 2):
                    dve.wait_ge(hlo_done, c - 1)
                v.tensor_tensor(hid[:, n % 2, :], act_g[:, n % 2, :], u_ps[n % 2][:], ALU.mult).then_inc(hid_done, 1)
                if not (first and n == 0):
                    rest(t, n - 1)
                if n % 2 == 0 and n // 2 + 1 <= E:
                    k = n // 2 + 1
                    dve.wait_ge(xwhi_done, t * E + k)
                    v.tensor_tensor(xw_lo[:, k % 2, :], xw_ps[:], xw_hi[:, k % 2, :].bitcast(F32),
                                    ALU.subtract).then_inc(xwlo_done, 1)

            def rest(t, n):
                dve.wait_ge(hhi_done, t * NCH + n + 1)
                v.tensor_tensor(h_lo[:, n % 3, :], hid[:, n % 2, :], h_hi[:, n % 3, :].bitcast(F32),
                                ALU.subtract).then_inc(hlo_done, 1)

            def prep_at(stage):
                def prep(t, par, n):
                    tl = t - stage * NT
                    if n == 4:
                        if stage == 0:
                            dve.wait_ge(x_loaded, tl * 16 + 16)
                        for j in range(SUB):
                            ins = v.bn_stats(st[:, j, :], x_sb[:, bass.ds(tl * SUB + j, 1), :].rearrange("p a d -> p (a d)"))
                        self_.done(ins, apart=passed)
                        for j in range(SUB):
                            ins = v.bn_aggr(mv[:, j, :], st[:, j, :])
                        ins.then_inc(stats_done, 1)
                    if n == 5:
                        dve.wait_ge(rstd_done, t + 1)
                        for j in range(SUB):
                            ins = v.tensor_scalar(xn[:, par, j, :],
                                                  x_sb[:, bass.ds(tl * SUB + j, 1), :].rearrange("p a d -> p (a d)"),
                                                  mv[:, j, 0:1], rstd[:, j:j + 1], ALU.subtract, ALU.mult)
                        ins.then_inc(xn_done, 1)
                    if n == 7:
                        dve.wait_ge(xhi_done, t + 1)
                        v.tensor_tensor(x_lo[:, par, :], prep_ps[:], x_hi[:, par, :].bitcast(F32),
                                        ALU.subtract).then_inc(xlo_done, 1)
                    if n == 9:
                        dve.wait_ge(logits_done, t + 1)
                        lg = fin_ps[:, 0:SUB * E].rearrange("p (j e) -> p j e", j=SUB)
                        self_.done(v.tensor_reduce(lmax[:], lg, AX.X, ALU.max))
                        v.tensor_tensor(lsub[:], lg, lmax[:].rearrange("p (j a) -> p j a", a=1).broadcast_to((P, SUB, E)),
                                        ALU.subtract).then_inc(lsub_done, 1)
                    if n == 11:
                        gate(t, par)
                return prep

            def gate(t, par):
                dve.wait_ge(lsub_done, t + 1)
                if not (isinstance(t, int) and t == 0):
                    dve.wait_ge(wtok_done, t)
                pj = [lsub[:, j:j + 1, :].broadcast_to((P, E, E)) for j in range(SUB)]
                pe_ = [lsub[:, j, :].rearrange("p (e a) -> p e a", a=1).broadcast_to((P, E, E)) for j in range(SUB)]
                for j in range(SUB):
                    v.tensor_tensor(cmp_ge[:, j], pj[j], pe_[j], ALU.is_ge)
                for j in range(SUB):
                    ins = v.tensor_tensor(cmp_gt[:, j], pj[j], pe_[j], ALU.is_gt)
                self_.done(ins)
                flat = lambda a: a[:].rearrange("p j e f -> p j (e f)")
                over = lambda a: a[:].rearrange("p (o e) f -> p o (e f)", o=1).broadcast_to((P, SUB, E * E))
                self_.done(v.tensor_tensor(flat(cmp_ge), flat(cmp_ge), over(before), ALU.mult))
                self_.done(v.tensor_tensor(flat(cmp_gt), flat(cmp_gt), over(after), ALU.mult))
                self_.done(v.tensor_tensor(flat(cmp_ge), flat(cmp_ge), flat(cmp_gt), ALU.add))
                self_.done(v.tensor_reduce(rank[:], cmp_ge[:], AX.X, ALU.add))
                dve.wait_ge(tanh_done, t + 1)
                self_.done(v.tensor_scalar(th1[:], th[:], -1.0, 1.0, ALU.mult, ALU.add))
                self_.done(v.reciprocal(th1[:], th1[:]))
                self_.done(v.scalar_tensor_tensor(out=prob[:], in0=th[:], scalar=1.0, in1=th1[:],
                                                  op0=ALU.add, op1=ALU.mult))
                self_.done(v.tensor_reduce(total[:], prob[:], AX.X, ALU.add))
                self_.done(v.scalar_tensor_tensor(out=chosen[:], in0=rank[:], scalar=2.0, in1=prob[:],
                                                  op0=ALU.is_lt, op1=ALU.mult))
                self_.done(v.tensor_reduce(top2[:], chosen[:], AX.X, ALU.add))
                self_.done(v.scalar_tensor_tensor(out=top2[:], in0=total[:], scalar=1e-20, in1=top2[:],
                                                  op0=ALU.mult, op1=ALU.add))
                self_.done(v.reciprocal(rtop[:], top2[:]))
                v.tensor_tensor(w_tok[:, par], chosen[:],
                                rtop[:].rearrange("p (j a) -> p j a", a=1).broadcast_to((P, SUB, E)),
                                ALU.mult).then_inc(wtok_done, 1)

            def finish_at(stage):
                def finish(t, par, last):
                    tl = t - stage * NT
                    dve.wait_ge(yT_done, t + 1)
                    xs = x_sb[:, bass.ds(tl * SUB, SUB), :].rearrange("p j d -> p (j d)")
                    v.tensor_tensor(xs, xs, fin_ps[:], ALU.add).then_inc(xnew_done, 1)
                return finish

            def tail(t, par):
                rest(t, NCH - 1)

            def piece(b, p, slot, scores, late, tail, ahead):
                if late and slot == 0:
                    maxima(b - 1, 1 - p)
                if ahead:
                    project(b + 1, 1 - p, slot)
                if scores and slot == 6:
                    gated_values(b, p)
                if scores and slot == 0 and not (isinstance(b, int) and b == 0):
                    dve.wait_ge(m_done, b)
                if scores and slot in S_SLOT:
                    n = S_SLOT[slot]
                    half, rep, c = S_UNITS[n]
                    dve.wait_ge(s_done, b * UNITS + n + 1)
                    v.tensor_reduce(mx[:, c, half, rep, :], s_ps[n % 2][:].rearrange("p (r k) -> p r k", r=KVH),
                                    AX.X, ALU.max).then_inc(max_done, 1)
                if late and slot in (17, 23):
                    normalise((b - 1) * 4 + (slot - 17) // 6, (slot - 17) // 6)
                if tail and slot == 1:
                    normalise((b - 2) * 4 + 2, 2)
                if tail and slot == 7:
                    normalise((b - 2) * 4 + 3, 3)
                if tail and slot == 8:
                    combine(b - 2)
                if tail and slot == 11:
                    dve.wait_ge(yahi_done, b - 1)
                    v.tensor_tensor(ya_lo[:], e_ps[:, 0:2 * P], ya_hi[:].bitcast(F32), ALU.subtract).then_inc(yalo_done, 1)
                if tail and slot == 13:
                    dve.wait_ge(wo_done, b - 1)
                    xs = x_sb[:, bass.ds((b - 2) * 2, 2), :].rearrange("p j d -> p (j d)")
                    v.tensor_tensor(xs, xs, e_ps[:, 2 * P:4 * P], ALU.add).then_inc(att_done, 1)

            def gated_values(b, p):
                dve.wait_ge(a_eg, b + 1)
                if not (isinstance(b, int) and b < 2):
                    dve.wait_ge(pv_done, (b - 1) * 4)
                self_.done(v.tensor_scalar(eg[:], eg[:], 1.0, None, ALU.add))
                self_.done(v.reciprocal(eg[:], eg[:]))
                for j in range(2):
                    vv = qkv[:, j, NH * HD:NH * HD + KVH * HD].rearrange("p (r d) -> p r d", r=KVH)
                    gg = eg[:, j, :].rearrange("p (r d) -> p r d", r=KVH)
                    for half in range(2):
                        d = slice(HALF * half, HALF * half + HALF)
                        ins = v.tensor_tensor(v1[:, p, j, half, :, 0:HALF], vv[:, :, d], gg[:, :, d], ALU.mult)
                ins.then_inc(a_v, 1)

            def maxima(b, p):
                dve.wait_ge(max_done, (b + 1) * UNITS)
                flat = mx[:].rearrange("p c h i r -> p c (h i r)")
                self_.done(v.tensor_tensor(flat[:, 1, :], flat[:, 1, :], flat[:, 2, :], ALU.max))
                m = flat[:, 0:2, :].rearrange("p c g -> p (c g)")
                st_ = qs[:, p].rearrange("p j h i r c -> p (j h i r) c")
                self_.done(v.tensor_scalar(st_[:, :, 12].bitcast(F32R), m, -1.0, None, ALU.mult))
                v.scalar_tensor_tensor(out=st_[:, :, 13], in0=m, scalar=-1.0, in1=st_[:, :, 12],
                                       op0=ALU.mult, op1=ALU.subtract).then_inc(m_done, 1)

            def project(b, p, slot):
                if slot == 1:
                    for j in range(2):
                        ins = v.bn_stats(ast[:, j, :], x_sb[:, bass.ds(b * 2 + j, 1), :].rearrange("p a d -> p (a d)"))
                    self_.done(ins, apart=passed)
                    for j in range(2):
                        ins = v.bn_aggr(amv[:, j, :], ast[:, j, :])
                    ins.then_inc(a_stats, 1)
                if slot == 2:
                    dve.wait_ge(a_rstd, b + 1)
                    for j in range(2):
                        ins = v.tensor_scalar(xa[:, j, :], x_sb[:, bass.ds(b * 2 + j, 1), :].rearrange("p a d -> p (a d)"),
                                              amv[:, j, 0:1], arstd[:, j:j + 1], ALU.subtract, ALU.mult)
                    ins.then_inc(a_xn, 1)
                if slot == 4:
                    dve.wait_ge(a_xhi, b + 1)
                    v.tensor_tensor(xa_lo[:], a_ps[:, 0:2 * P], xa_hi[:].bitcast(F32), ALU.subtract).then_inc(a_xlo, 1)
                qk = qkv[:, :, 0:NH * HD].rearrange("p j (h d) -> p j h d", h=NH)
                if slot == 9:
                    dve.wait_ge(a_qkv, b + 1)
                    self_.done(v.tensor_tensor(sq[:].rearrange("p j h d -> p j (h d)"), qkv[:, :, 0:NH * HD],
                                               qkv[:, :, 0:NH * HD], ALU.mult))
                    v.tensor_reduce(ms[:], sq[:], AX.X, ALU.add).then_inc(a_ms, 1)
                if slot == 13:
                    dve.wait_ge(a_rq, b + 1)
                    if not (isinstance(b, int) and b == 0):
                        dve.wait_ge(a_stack, 2 * b)
                    for j in range(2):
                        ins = v.tensor_tensor(qn[:, j], qk[:, j],
                                              rq[:, j, :].rearrange("p (h a) -> p h a", a=1).broadcast_to((P, NH, HD)),
                                              ALU.mult)
                    self_.done(ins)
                if slot in (14, 15):
                    j = slot - 14
                    one = lambda a, n: a.rearrange("p (a d) -> p a d", a=1).broadcast_to((P, NH, n))
                    v.tensor_tensor(ra[:, j], qn[:, j], one(cc[:, j, :], HD), ALU.mult)
                    v.tensor_tensor(rb[:, j, :, 0:HALF], qn[:, j, :, HALF:HD], one(ss[:, j, 0:HALF], HALF), ALU.mult)
                    ins = v.tensor_tensor(rb[:, j, :, HALF:HD], qn[:, j, :, 0:HALF], one(ss[:, j, HALF:HD], HALF), ALU.mult)
                    if j == 1:
                        self_.done(ins)
                if slot == 16:
                    self_.done(v.tensor_tensor(ra[:].rearrange("p j h d -> p (j h d)"), ra[:].rearrange("p j h d -> p (j h d)"),
                                               rb[:].rearrange("p j h d -> p (j h d)"), ALU.add))
                if slot in (17, 18, 19, 20):
                    half, j = (slot - 17) // 2, (slot - 17) % 2
                    if slot == 17:
                        if not (isinstance(b, int) and b == 0):
                            dve.wait_ge(a_kT, 2 * b)
                        if not (isinstance(b, int) and b < 2):
                            dve.wait_ge(q2T_done, (b - 1) * 4)
                        st_ = qs[:, p].rearrange("p j h i r c -> p (j h i r) c")
                        v.memset(st_[:, :, 12:14], 0.0)
                    d = slice(HALF * half, HALF * half + HALF)
                    rq_ = ra[:, j, 0:HEADS].rearrange("p (r i) d -> p i r d", i=REP)[:, :, :, d]
                    rk_ = ra[:, j, HEADS:NH][:, :, d]
                    qs_, ks_ = qs[:, p, j, half], ks[:, j, half]
                    v.tensor_copy(qs_[:, :, :, 0:4].bitcast(F32R), rq_)
                    v.tensor_copy(qs_[:, :, :, 4:8].bitcast(F32R), rq_)
                    v.tensor_copy(ks_[:, :, 0:4].bitcast(F32R), rk_)
                    self_.done(v.tensor_copy(ks_[:, :, 8:12].bitcast(F32R), rk_))
                    v.tensor_tensor(qs_[:, :, :, 8:12], rq_, qs_[:, :, :, 0:4], ALU.subtract)
                    ins = v.tensor_tensor(ks_[:, :, 4:8], rk_, ks_[:, :, 0:4], ALU.subtract)
                    if j == 1:
                        ins.then_inc(a_stack, 1)

            def normalise(count, hp):
                dve.wait_ge(oT_done, count + 1)
                o = e_ps[:].rearrange("p (g c) -> p g c", c=GRP)
                self_.done(v.reciprocal(rden[:], o[:, :, HALF]))
                v.tensor_tensor(an[:, hp // 2, hp % 2], o[:, :, 0:HALF],
                                rden[:].rearrange("p (g a) -> p g a", a=1).broadcast_to((P, 16, HALF)),
                                ALU.mult).then_inc(an_done, 1)

            def combine(b):
                dve.wait_ge(an_done, (b + 1) * 4)
                flat = an[:].rearrange("p h i g d -> p h (i g d)")
                self_.done(v.tensor_tensor(lt[:], flat[:, 1, :], lam_x[:].rearrange("p i j r d -> p (i j r d)"), ALU.mult))
                a1 = flat[:, 0, :].rearrange("p (i j r d) -> p j i r d", i=REP, j=2, r=KVH)
                l2 = lt[:].rearrange("p (i j r d) -> p j i r d", i=REP, j=2, r=KVH)
                for j in range(2):
                    yo = ya[:, j].rearrange("p (r i) d -> p i r d", i=REP)
                    v.tensor_tensor(yo[:, :, :, 0:HALF], a1[:, j], l2[:, j], ALU.subtract)
                    ins = v.tensor_tensor(yo[:, :, :, HALF:HD], a1[:, j], l2[:, j], ALU.add)
                ins.then_inc(ya_done, 1)

            ffn_stage(0, step, prep_at(0), finish_at(0), tail, [self_], 2 * DVE_FFN)
            attention(piece, 2 * DVE_ATT, [self_])
            dve.wait_ge(att_done, BATCH)
            ffn_stage(1, step, prep_at(1), finish_at(1), tail, [self_], 2 * DVE_FFN)

        @block.tensor
        def _(pe):
            t_ = nc.tensor
            engine_of[0] = pe
            pe.wait_ge(consts, N_CONST)
            pe.wait_ge(w_lo_done, 2 + E + 1)

            def product(o, w_h, w_l, m_h, m_l, start=True, stop=True):
                t_.matmul(o, w_h, m_h, start=start, stop=False)
                t_.matmul(o, w_l, m_h, start=False, stop=False)
                return t_.matmul(o, w_h, m_l, start=False, stop=stop)

            def step(t, n, par, first, last):
                c = t * NCH + n
                e, h = ORDER[n // 2], (n % 2) * P
                zero = isinstance(t, int) and t == 0
                if n == 0:
                    pe.wait_ge(xhi_done, t + 1)
                    pe.wait_ge(xlo_done, t + 1)
                if not (zero and n < 2):
                    pe.wait_ge(silu_done, c - 1)
                product(g_ps[n % 2][:], w_hi[:, e, 0, h:h + P], w_lo[:, e, 0, h:h + P],
                        x_hi[:, par, :], x_lo[:, par, :]).then_inc(g_done, 1)
                if not (zero and n < 2):
                    pe.wait_ge(hid_done, c - 1)
                k = n // 2
                if k:
                    pe.wait_ge(xwhi_done, t * E + k)
                    pe.wait_ge(xwlo_done, t * E + k)
                    mh, ml = xw_hi[:, k % 2, :], xw_lo[:, k % 2, :]
                else:
                    mh, ml = x_hi[:, par, :], x_lo[:, par, :]
                product(u_ps[n % 2][:], w_hi[:, e, 1, h:h + P], w_lo[:, e, 1, h:h + P], mh, ml).then_inc(u_done, 1)
                if n % 2 == 0 and n // 2 + 1 <= E:
                    k = n // 2 + 1
                    pe.wait_ge(xw_done, t * E + k)
                    if not (zero and k == 1):
                        pe.wait_ge(xwlo_done, t * E + k - 1)
                    for j in range(SUB):
                        ins = t_.transpose(xw_ps[:, j * P:(j + 1) * P], xw[:, k % 2, j, :], ident[:])
                    ins.then_inc(xwT_done, 1)
                if n >= 2 or not first:
                    down(t, n - 2) if n >= 2 else down(t - 1, n - 2 + NCH)

            def down(t, n):
                c = t * NCH + n
                e, q = ORDER[n // 2], (n % 2) * P
                pe.wait_ge(hhi_done, c + 1)
                pe.wait_ge(hlo_done, c + 1)
                if n == 0 and not (isinstance(t, int) and t == 0):
                    pe.wait_ge(y_done, t)
                product(y_ps[:], w_hi[:, e, 2, q:q + P], w_lo[:, e, 2, q:q + P], h_hi[:, n % 3, :], h_lo[:, n % 3, :],
                        start=n == 0, stop=n == NCH - 1).then_inc(down_done, 1)

            def prep(t, par, n):
                if n == 6:
                    pe.wait_ge(xn_done, t + 1)
                    for j in range(SUB):
                        ins = t_.transpose(prep_ps[:, j * P:(j + 1) * P], xn[:, par, j, :], ident[:])
                    ins.then_inc(xnT_done, 1)
                if n == 8:
                    pe.wait_ge(xhi_done, t + 1)
                    pe.wait_ge(xlo_done, t + 1)
                    for j in range(SUB):
                        q = slice(j * P, (j + 1) * P)
                        ins = product(fin_ps[:, j * E:(j + 1) * E], x_hi[:, par, q], x_lo[:, par, q], gw_hi[:], gw_lo[:])
                    ins.then_inc(logits_done, 1)

            def tail(t, par):
                down(t, NCH - 2)
                down(t, NCH - 1)

            def finish(t, par, last):
                pe.wait_ge(y_done, t + 1)
                pe.wait_ge(lsub_done, t + 1 if last else t + 2)
                for j in range(SUB):
                    ins = t_.transpose(fin_ps[:, j * P:(j + 1) * P], y_sb[:, j * P:(j + 1) * P], ident[:])
                ins.then_inc(yT_done, 1)

            def piece(b, p, slot, scores, late, tail, ahead):
                if late and slot in (2, 4, 6, 8):
                    hp = (slot - 2) // 2
                    pe.wait_ge(m_done, b)
                    if hp:
                        pe.wait_ge(q2_done, (b - 1) * 4 + hp)
                    else:
                        pe.wait_ge(a_q1, min_q1(b))
                    ins = turn_queries(1 - p, hp)
                    ins.then_inc(q2T_done, 1)
                if ahead:
                    project(b + 1, 1 - p, slot, late)
                if scores and slot in S_SLOT:
                    n = S_SLOT[slot]
                    half, rep, c = S_UNITS[n]
                    qt, kt, edge = COMBOS[c]
                    pe.wait_ge(a_q1, b * 4 + half * 2 + rep // 2 + 1)
                    pe.wait_ge(a_kb, b * 2 + half + 1)
                    if not (isinstance(b, int) and b == 0 and n < 2):
                        pe.wait_ge(max_done, b * UNITS + n - 1)
                    o = s_ps[n % 2][:].rearrange("p (r k) -> p r k", r=KVH)
                    if edge:
                        t_.matmul(o, ident_b[:], mask_b[:], start=True, stop=False)
                    t_.matmul(o, q1[:, p, half, rep, qt * P:(qt + 1) * P], kb[:, p, half, :, kt * P:(kt + 1) * P],
                              start=not edge, stop=True).then_inc(s_done, 1)
                u = slot - T_LAG
                if late and u >= 0:
                    hp, j = u // 6, u % 6
                    half, i0 = hp // 2, 2 * (hp % 2)
                    if j == 0:
                        pe.wait_ge(q2_done, (b - 1) * 4 + hp + 1)
                    if not (isinstance(b, int) and b == 1 and u < 2):
                        pe.wait_ge(exp_done, (b - 1) * UNITS + u - 1)
                    if j < 4:
                        ins = t_.matmul(t_ps[u % 2][:], kb[:, 1 - p, half, j, 0:P], q2[:, half, i0:i0 + 2, :],
                                        start=True, stop=True)
                    else:
                        for r in (2 * (j - 4), 2 * (j - 4) + 1):
                            ins = t_.matmul(t_ps[u % 2][:, (r % 2) * 256:(r % 2) * 256 + 256],
                                            kb[:, 1 - p, half, r, P:2 * P], q2[:, half, i0:i0 + 2, P:2 * P],
                                            start=True, stop=True)
                    ins.then_inc(t_done, 1)
                if late and slot in (12, 18, 24):
                    values(b - 1, (slot - 12) // 6, 1 - p, isinstance(b, int) and b == 1)
                if late and slot in (16, 22):
                    turn_outputs((b - 1) * 4 + (slot - 16) // 6, (slot - 16) // 6, isinstance(b, int) and b == 1, b)
                if tail and slot == 0:
                    turn_outputs((b - 2) * 4 + 2, 2, False, b)
                if tail and slot == 2:
                    values(b - 2, 3, p, False)
                if tail and slot == 6:
                    turn_outputs((b - 2) * 4 + 3, 3, False, b)
                if tail and slot == 9:
                    pe.wait_ge(ya_done, b - 1)
                    pe.wait_ge(an_done, (b - 1) * 4)
                    for j in range(2):
                        ins = t_.transpose(e_ps[:, j * P:(j + 1) * P], ya[:, j].rearrange("p h d -> p (h d)"), ident[:])
                    ins.then_inc(yaT_done, 1)
                if tail and slot == 12:
                    pe.wait_ge(yahi_done, b - 1)
                    pe.wait_ge(yalo_done, b - 1)
                    for j in range(2):
                        q = slice(j * P, (j + 1) * P)
                        ins = product(e_ps[:, (2 + j) * P:(3 + j) * P], ya_hi[:, q], ya_lo[:, q], wa_hi[:, QKV:], wa_lo[:, QKV:])
                    ins.then_inc(wo_done, 1)

            def min_q1(b):
                if isinstance(b, int):
                    return min(4 * (b + 1), 4 * BATCH)
                return b * 4 + 4

            def turn_queries(p, hp):
                half, i0 = hp // 2, 2 * (hp % 2)
                for i in range(2):
                    for j in range(2):
                        o = (2 * i + j) * P
                        ins = t_.transpose(qT_ps[:, o:o + P], qs[:, p, j, half, i0 + i].rearrange("p r c -> p (r c)"), ident[:])
                return ins

            def project(b, p, slot, late):
                if slot == 3:
                    pe.wait_ge(a_xn, b + 1)
                    if not (isinstance(b, int) and b == 0):
                        pe.wait_ge(a_kb, b * 2)
                    for j in range(2):
                        ins = t_.transpose(a_ps[:, j * P:(j + 1) * P], xa[:, j, :], ident[:])
                    ins.then_inc(a_xnT, 1)
                if slot == 6:
                    pe.wait_ge(a_xhi, b + 1)
                    pe.wait_ge(a_xlo, b + 1)
                    for j in range(2):
                        q = slice(j * P, (j + 1) * P)
                        ins = product(a_ps[:, j * QKV:(j + 1) * QKV], xa_hi[:, q], xa_lo[:, q], wa_hi[:, 0:QKV], wa_lo[:, 0:QKV])
                    ins.then_inc(a_proj, 1)
                if slot in (20, 24):
                    half = (slot - 20) // 4
                    pe.wait_ge(a_stack, 2 * b + half + 1)
                    if half:
                        pe.wait_ge(a_kb, 2 * b + 1)
                    else:
                        pe.wait_ge(a_eg, b + 1)
                    for j in range(2):
                        o = (2 * half + j) * P
                        ins = t_.transpose(a_ps[:, o:o + P], ks[:, j, half].rearrange("p r c -> p (r c)"), ident[:])
                    ins.then_inc(a_kT, 1)
                if slot in (19, 21, 23, 25):
                    hp = (slot - 19) // 2
                    pe.wait_ge(a_stack, 2 * b + hp // 2 + 1)
                    if hp:
                        pe.wait_ge(a_q1, b * 4 + hp)
                    elif late:
                        pe.wait_ge(q2_done, (b - 1) * 4)
                    turn_queries(p, hp).then_inc(a_q1T, 1)

            def values(batch, hp, p, fresh):
                count, half = batch * 4 + hp, hp // 2
                pe.wait_ge(sel_done, (count + 1) * 6)
                pe.wait_ge(a_v, batch + 1)
                if not (fresh and hp == 0):
                    pe.wait_ge(o_done, count)
                for r in range(KVH):
                    t_.matmul(o_ps[GRP * r:GRP * r + GRP, :], v1[:, p, 0, half, r, :], pr[:, hp % 2, r, :],
                              start=True, stop=False)
                for r in range(KVH):
                    ins = t_.matmul(o_ps[GRP * r:GRP * r + GRP, :].rearrange("p (i q) -> p i q", i=2)[:, :, P:2 * P],
                                    v1[:, p, 1, half, r, :],
                                    pr[:, hp % 2, 4 + r // 2, (r % 2) * 256:(r % 2) * 256 + 256].rearrange("p (i q) -> p i q", i=2),
                                    start=False, stop=True)
                ins.then_inc(pv_done, 1)

            def turn_outputs(count, hp, fresh, b):
                pe.wait_ge(o_done, count + 1)
                if not (fresh and hp == 0):
                    pe.wait_ge(an_done, count)
                if hp == 0 and not fresh and not (isinstance(b, int) and b < 2):
                    pe.wait_ge(att_done, b - 1)
                for i in range(4):
                    ins = t_.transpose(e_ps[:, i * P:(i + 1) * P], o_sb[:, hp % 2, i * P:(i + 1) * P], ident[:])
                ins.then_inc(oT_done, 1)

            ffn_stage(0, step, prep, finish, tail)
            pe.wait_ge(xnew_done, NT)
            pe.wait_ge(xwlo_done, NT * E)
            attention(piece)
            pe.wait_ge(att_done, BATCH)
            pe.wait_ge(a_kb, 2 * BATCH)
            pe.wait_ge(exp_done, BATCH * UNITS)
            pe.wait_ge(max_done, BATCH * UNITS)
            ffn_stage(1, step, prep, finish, tail)


DVE_FFN = 15
DVE_ATT = 18



def kernel(**inputs):
    import numpy as np
    import concourse.bacc as bacc
    from concourse.bass_utils import run_bass_kernel_spmd

    g = {k: np.asarray(v) for k, v in inputs.items()}
    angles = np.arange(0, HD, 2, dtype=np.float32) / np.float32(HD) * np.float32(np.pi)
    pos = np.arange(SEQ, dtype=np.float32)
    radius = np.float32(1.0) / (np.float32(1.0) + pos[:, None] * np.float32(0.01))
    ang = (pos[:, None] * angles[None, :]).astype(np.float32)
    rot = np.stack([radius * np.cos(ang.astype(np.float64)).astype(np.float32),
                    radius * np.sin(ang.astype(np.float64)).astype(np.float32)], axis=1).astype(np.float32)
    send = {
        "x": g["L0_attn_x"], "w_gate": g["L0_ffn_w_gate"], "w_up": g["L0_ffn_w_up"], "w_down": g["L0_ffn_w_down"],
        "ws_gate": g["L0_ffn_ws_gate"], "ws_up": g["L0_ffn_ws_up"], "ws_down": g["L0_ffn_ws_down"],
        "gate_w": g["L0_ffn_gate_w"],
        "wqkv": np.concatenate([g["L0_attn_Wq"], g["L0_attn_Wk"], g["L0_attn_Wv"], g["L0_attn_Wg"]], axis=0).T,
        "wo": g["L0_attn_Wo"].T, "q_gain": g["L0_attn_q_gain"], "lam": g["L0_attn_lambda_param"], "rot": rot,
    }
    nc = bacc.Bacc("TRN2", target_bir_lowering=False, num_devices=1)
    arrays, args = {}, []
    for name, a in send.items():
        a = np.ascontiguousarray(a)
        arrays[f"in_{name}_dram"] = a
        args.append(nc.dram_tensor(f"in_{name}_dram", a.shape, mybir.dt.from_np(a.dtype), kind="ExternalInput").ap())
    o = nc.dram_tensor("out_0_dram", (BATCH, SEQ, DIM), F32, kind="ExternalOutput").ap()
    macaron(nc, *args, o)
    r = run_bass_kernel_spmd(nc, [arrays], core_ids=[0])
    return r.results[0]["out_0_dram"]
```

```python
from contextlib import ExitStack

import concourse.bass as bass
from concourse import mybir

F32 = mybir.dt.float32
F32R = mybir.dt.float32r
BF16 = mybir.dt.bfloat16
ALU = mybir.AluOpType
ACT = mybir.ActivationFunctionType
AX = mybir.AxisListType

P = 128
BATCH, SEQ, DIM = 16, 256, 128
TOKT = BATCH * SEQ // P
TILE = 512
SUB = TILE // P
NT = BATCH * SEQ // TILE
E, HID = 8, 256
NCH = (E + 1) * 2
LEAD = 4
HEADS, KVH, HD = 16, 4, 8
HALF = HD // 2
REP = HEADS // KVH
QKV = DIM + 3 * KVH * HD
NH = HEADS + KVH
GRP = 32
LN_EPS = 1e-5
RMS_EPS = 1.1920928955078125e-07
NEG = -1.0e30
UNITS = 24
T_LAG = 4
SLOTS = UNITS + T_LAG


class Links:

    def __init__(self, engine, sem):
        self.engine, self.sem, self.base, self.n = engine, sem, 0, 0

    def done(self, ins, apart=None):
        self.n += 1
        ins.then_inc(self.sem, 1)
        if apart:
            wait_apart(self.engine, self.sem, self.base + self.n, apart)
        else:
            self.engine.wait_ge(self.sem, self.base + self.n)

    def enter(self, i, per):
        self.start, self.per = self.base + self.n, per
        self.base, self.n = self.start + i * per, 0

    def leave(self, times):
        assert self.n == self.per, f"{self.n} steps in the body, not {self.per}"
        self.base, self.n = self.start + times * self.per, 0


def wait_apart(engine, sem, value, passed):
    engine.wait_ge(sem, value)
    engine.sem_inc(passed, 1)


def macaron(nc, x_in, w_gate, w_up, w_down, ws_gate, ws_up, ws_down, gate_w, wqkv, wo, q_gain, lam, rot, out):
    ctx = ExitStack()
    with ctx:
        def sb(name, shape, dt=F32):
            return ctx.enter_context(nc.sbuf_tensor(name, shape, dt))

        def sem(name):
            return ctx.enter_context(nc.semaphore(name))

        bank = [ctx.enter_context(nc.psum_tensor(f"bank{i}", [P, 512], F32)) for i in range(8)]
        g_ps, u_ps, y_ps, xw_ps, prep_ps, fin_ps = bank[0:2], bank[2:4], bank[4], bank[5], bank[6], bank[7]
        s_ps, t_ps, o_ps, a_ps, qT_ps, e_ps = bank[0:2], bank[2:4], bank[4], bank[5], bank[6], bank[7]

        x_sb = sb("x_sb", [P, TOKT, DIM])
        w_raw = sb("w_raw", [P, E + 1, 3, HID])
        w_hi = sb("w_hi", [P, E + 1, 3, HID], F32R)
        w_lo = sb("w_lo", [P, E + 1, 3, HID], F32R)
        pr = w_raw[:].rearrange("p e j d -> p (e j d)")[:, 0:6144].rearrange("p (a j n) -> p a j n", a=2, j=6)
        arena = sb("arena", [P, 7168], F32R)

        def cut(at, *dims):
            size = 1
            for d in dims:
                size *= d
            names_ = "abcd"[:len(dims)]
            flat = arena[:, at:at + size]
            return flat.rearrange(f"p ({' '.join(names_)}) -> p {' '.join(names_)}", **dict(zip(names_, dims)))

        gw_raw, gw_hi, gw_lo = sb("gw_raw", [P, E]), sb("gw_hi", [P, E], F32R), sb("gw_lo", [P, E], F32R)
        wa_raw = sb("wa_raw", [P, QKV + DIM])
        wa_hi, wa_lo = sb("wa_hi", [P, QKV + DIM], F32R), sb("wa_lo", [P, QKV + DIM], F32R)
        ident = sb("ident", [P, P])
        ident_b = sb("ident_b", [P, P], BF16)
        mask_b = sb("mask_b", [P, KVH, P], BF16)
        minus_half = sb("minus_half", [P, 2 * NH])
        before = sb("before", [P, E, E])
        after = sb("after", [P, E, E])

        st = sb("st", [P, SUB, 6])
        mv = sb("mv", [P, SUB, 2])
        rstd = sb("rstd", [P, SUB])
        xn = sb("xn", [P, 2, SUB, DIM])
        x_hi, x_lo = cut(0, 2, TILE), cut(1024, 2, TILE)
        lmax = sb("lmax", [P, SUB])
        lsub = sb("lsub", [P, SUB, E])
        prob = sb("prob", [P, SUB, E])
        cmp_ge, cmp_gt = sb("cmp_ge", [P, SUB, E, E]), sb("cmp_gt", [P, SUB, E, E])
        rank, chosen = sb("rank", [P, SUB, E]), sb("chosen", [P, SUB, E])
        total, top2, rtop = sb("total", [P, SUB]), sb("top2", [P, SUB]), sb("rtop", [P, SUB])
        w_tok = sb("w_tok", [P, 2, SUB, E])
        xw = sb("xw", [P, 2, SUB, DIM])
        xw_hi, xw_lo = cut(2048, 2, TILE), cut(3072, 2, TILE)
        act_g = sb("act_g", [P, 2, TILE])
        hid = sb("hid", [P, 2, TILE])
        h_hi, h_lo = cut(4096, 3, TILE), cut(5632, 3, TILE)
        y_sb = sb("y_sb", [P, TILE])

        rot_sb = sb("rot_sb", [P, 2, 2, HALF])
        cc = sb("cc", [P, 2, HD])
        ss = sb("ss", [P, 2, HD])
        gain_in = sb("gain_in", [P, HEADS])
        lam_in = sb("lam_in", [P, HEADS])
        gain = sb("gain", [P, 2, NH])
        lam_x = sb("lam_x", [P, REP, 2, KVH, HALF])
        ast, amv, arstd = sb("ast", [P, 2, 6]), sb("amv", [P, 2, 2]), sb("arstd", [P, 2])
        xa = sb("xa", [P, 2, DIM])
        xa_hi, xa_lo = sb("xa_hi", [P, 2 * P], F32R), sb("xa_lo", [P, 2 * P], F32R)
        qkv = sb("qkv", [P, 2, QKV])
        eg = sb("eg", [P, 2, KVH * HD])
        sq = sb("sq", [P, 2, NH, HD])
        ms = sb("ms", [P, 2, NH])
        ma, r0, lnm = sb("ma", [P, 2, NH]), sb("r0", [P, 2, NH]), sb("lnm", [P, 2, NH])
        rq = sb("rq", [P, 2, NH])
        eps_col = sb("eps_col", [P, 1])
        th, th1 = sb("th", [P, SUB, E]), sb("th1", [P, SUB, E])
        qn = sb("qn", [P, 2, NH, HD])
        ra, rb = sb("ra", [P, 2, NH, HD]), sb("rb", [P, 2, NH, HD])
        qs = sb("qs", [P, 2, 2, 2, REP, KVH, GRP])
        ks = sb("ks", [P, 2, 2, KVH, GRP])
        q1 = cut(0, 2, 2, REP, SEQ)
        q2 = cut(4096, 2, REP, SEQ)
        kb = sb("kb", [P, 2, 2, KVH, SEQ], F32R)
        v1 = sb("v1", [P, 2, 2, 2, KVH, GRP])
        mx = sb("mx", [P, 3, 2, REP, KVH])
        o_sb = act_g
        rden = sb("rden", [P, 16])
        an = sb("an", [P, 2, 2, 16, HALF])
        ya = sb("ya", [P, 2, HEADS, HD])
        lt = sb("lt", [P, P])
        ya_hi, ya_lo = sb("ya_hi", [P, 2 * P], F32R), sb("ya_lo", [P, 2 * P], F32R)

        names = """x_loaded gw_loaded small_loaded x_stored consts att_consts w_hi_done w_lo_done
            stats_done rstd_done xn_done xnT_done xhi_done xlo_done logits_done lsub_done tanh_done
            wtok_done xw_done xwT_done xwhi_done xwlo_done g_done u_done silu_done hid_done hhi_done
            hlo_done down_done y_done yT_done xnew_done dve_self pool_self
            a_stats a_rstd a_xn a_xnT a_xhi a_xlo a_proj a_qkv a_eg a_ms a_r0 a_rq act_self a_v a_stack a_kT a_kb
            a_q1T a_q1 s_done max_done m_done q2T_done q2_done t_done exp_done sel_done pv_done
            o_done oT_done an_done ya_done yaT_done yahi_done yalo_done wo_done att_done passed""".split()
        S = {n: sem(n) for n in names}
        (x_loaded, gw_loaded, small_loaded, x_stored, consts, att_consts, w_hi_done, w_lo_done,
         stats_done, rstd_done, xn_done, xnT_done, xhi_done, xlo_done, logits_done, lsub_done, tanh_done,
         wtok_done, xw_done, xwT_done, xwhi_done, xwlo_done, g_done, u_done, silu_done, hid_done, hhi_done,
         hlo_done, down_done, y_done, yT_done, xnew_done, dve_self, pool_self,
         a_stats, a_rstd, a_xn, a_xnT, a_xhi, a_xlo, a_proj, a_qkv, a_eg, a_ms, a_r0, a_rq, act_self, a_v, a_stack, a_kT, a_kb,
         a_q1T, a_q1, s_done, max_done, m_done, q2T_done, q2_done, t_done, exp_done, sel_done, pv_done,
         o_done, oT_done, an_done, ya_done, yaT_done, yahi_done, yalo_done, wo_done, att_done, passed) = [S[n] for n in names]

        GROUPS = [[E], [0], [1, 2], [3, 4], [5, 6, 7]]
        w_loaded = [sem(f"w_loaded{n}") for n in range(len(GROUPS))]

        ORDER = [E] + list(range(E))
        x_tok = x_in.rearrange("b (j p) d -> p (b j) d", p=P)
        out_tok = out.rearrange("b (j p) d -> p (b j) d", p=P)
        N_CONST = 4
        N_ATT = 5
        N_SMALL = 5

        SPLIT_AT = {6: [0], 9: [1], NCH: [2], NCH + 1: [3], NCH + 2: [4], NCH + 3: [5, 6, 7, 8]}

        def expert_lo(m):
            return m + 2

        block = ctx.enter_context(nc.Block())

        def nothing(*a):
            pass

        def ffn_stage(stage, step, prep, finish, tail, links=None, per=0, early=nothing):
            t0 = stage * NT

            def tile(t, par, last):
                for n in range(LEAD, NCH):
                    step(t, n, par, False, last)
                    if not last:
                        prep(t + 1, 1 - par, n)
                if not last:
                    for n in range(LEAD):
                        step(t + 1, n, 1 - par, False, False)
                    finish(t, par, last)
                else:
                    tail(t, par)
                    finish(t, par, last)

            for n in range(LEAD, NCH):
                prep(t0, 0, n)
                early(n)
            for n in range(LEAD):
                step(t0, n, 0, True, False)
                early(NCH + n)
            with (links[0].engine if links else engine_of[0]).Fori(0, NT // 2 - 1) as i:
                if links:
                    for li in links:
                        li.enter(i, per)
                tile(t0 + 2 * i, 0, False)
                tile(t0 + 2 * i + 1, 1, False)
            if links:
                for li in links:
                    li.leave(NT // 2 - 1)
            tile(t0 + NT - 2, 0, False)
            tile(t0 + NT - 1, 1, True)

        engine_of = [None]

        def attention(piece, per=0, links=None):
            def step(b, p, scores=True, late=True, tail=True, ahead=True):
                for slot in range(SLOTS):
                    piece(b, p, slot, scores, late, tail, ahead)

            def first():
                for slot in range(SLOTS):
                    piece(-1, 1, slot, False, False, False, True)
            first()
            step(0, 0, late=False, tail=False)
            step(1, 1, tail=False)
            loops = (BATCH - 4) // 2
            with (links[0].engine if links else engine_of[0]).Fori(0, loops) as i:
                if links:
                    for li in links:
                        li.enter(i, per)
                step(2 + 2 * i, 0)
                step(3 + 2 * i, 1)
            if links:
                for li in links:
                    li.leave(loops)
            step(BATCH - 2, 0)
            step(BATCH - 1, 1, ahead=False)
            step(BATCH, 0, scores=False, ahead=False)
            step(BATCH + 1, 1, scores=False, late=False, ahead=False)

        COMBOS = [(0, 0, True), (1, 0, False), (1, 1, True)]
        S_UNITS = [(half, rep, c) for half in range(2) for rep in range(REP) for c in range(3)]

        S_SLOT = {slot: n for n, slot in enumerate(x for x in range(SLOTS) if x not in (8, 16, 18, 21))}

        @block.sync
        def _(sp):
            sp.dma_start(x_sb[:, 0:SUB, :], x_tok[:, 0:SUB, :]).then_inc(x_loaded, 16)
            for n, group in enumerate(GROUPS):
                e, k = group[0], len(group)
                gates, ups = (ws_gate, ws_up) if e == E else (w_gate[e:e + k], w_up[e:e + k])
                for j, part in enumerate((gates, ups)):
                    src = part if e == E else part.rearrange("e p h -> p e h")
                    dst = w_raw[:, e, j, :] if e == E else w_raw[:, e:e + k, j, :]
                    sp.dma_start(dst, src).then_inc(w_loaded[n], 16)
                for e in group:
                    down = ws_down if e == E else w_down[e]
                    sp.dma_start(w_raw[:, e, 2, :].rearrange("p (c h) -> p c h", c=2),
                                 down.rearrange("(c p) h -> p c h", p=P)).then_inc(w_loaded[n], 16)
            with sp.Fori(1, NT) as t:
                wait_apart(sp, x_loaded, t * 16, passed)
                sp.dma_start(x_sb[:, bass.ds(t * SUB, SUB), :], x_tok[:, bass.ds(t * SUB, SUB), :]).then_inc(x_loaded, 16)
            with sp.Fori(0, NT) as t:
                sp.wait_ge(xnew_done, t + NT + 1)
                sp.dma_start(out_tok[:, bass.ds(t * SUB, SUB), :], x_sb[:, bass.ds(t * SUB, SUB), :]).then_inc(x_stored, 16)
            sp.wait_ge(x_stored, 16 * NT)

        @block.gpsimd
        def _(pool):
            self_ = Links(pool, pool_self)
            g = nc.gpsimd
            pool.dma_start(gw_raw[:], gate_w).then_inc(gw_loaded, 16)
            g.memset(minus_half[:], -0.5).then_inc(consts, 1)
            self_.done(g.memset(ident[:], 0.0))
            g.affine_select(out=ident[:], in_=ident[:], compare_op=ALU.not_equal, fill=1.0, base=0,
                            pattern=[[-1, P]], channel_multiplier=1).then_inc(consts, 1)

            def early(n):
                if n == 4:
                    self_.done(g.memset(before[:], 1.0))
                    self_.done(g.memset(after[:], 1.0))
                    g.affine_select(out=before[:], in_=before[:], compare_op=ALU.is_gt, fill=0.0, base=0,
                                    pattern=[[1, E], [-1, E]], channel_multiplier=0).then_inc(consts, 1)
                    g.affine_select(out=after[:], in_=after[:], compare_op=ALU.is_gt, fill=0.0, base=0,
                                    pattern=[[-1, E], [1, E]], channel_multiplier=0).then_inc(consts, 1)
                    pool.dma_start(wa_raw[:, 0:QKV], wqkv).then_inc(small_loaded, 16)
                    pool.dma_start(wa_raw[:, QKV:], wo).then_inc(small_loaded, 16)
                    pool.dma_start(rot_sb[:], rot.rearrange("(j p) a d -> p j a d", p=P)).then_inc(small_loaded, 16)
                    pool.dma_start(gain_in[:], q_gain.rearrange("(a h) -> a h", a=1).broadcast_to((P, HEADS))).then_inc(small_loaded, 16)
                    pool.dma_start(lam_in[:], lam.rearrange("(a h) -> a h", a=1).broadcast_to((P, HEADS))).then_inc(small_loaded, 16)
                if n == NCH + LEAD - 1:
                    self_.done(g.memset(ident_b[:], 0.0))
                    self_.done(g.memset(mask_b[:], 0.0))
                    g.affine_select(out=ident_b[:], in_=ident_b[:], compare_op=ALU.not_equal, fill=1.0, base=0,
                                    pattern=[[-1, P]], channel_multiplier=1).then_inc(att_consts, 1)
                    g.affine_select(out=mask_b[:], in_=mask_b[:], compare_op=ALU.is_ge, fill=NEG, base=0,
                                    pattern=[[0, KVH], [-1, P]], channel_multiplier=1).then_inc(att_consts, 1)
                    self_.done(g.memset(qs[:], 0.0))
                    self_.done(g.memset(ks[:], 0.0))
                    self_.done(g.memset(v1[:], 0.0))
                    g.memset(ks[:, :, :, :, 12:14], 1.0)
                    g.memset(v1[:, :, :, :, :, HALF:HALF + 1], 1.0)
                    g.memset(eps_col[:], RMS_EPS)
                    g.memset(kb[:].bitcast(F32), 0.0).then_inc(att_consts, 1)
                    pool.wait_ge(small_loaded, 16 * N_SMALL)
                    g.tensor_copy(cc[:, :, 0:HALF], rot_sb[:, :, 0, :])
                    g.tensor_copy(cc[:, :, HALF:HD], rot_sb[:, :, 0, :])
                    g.tensor_copy(ss[:, :, 0:HALF], rot_sb[:, :, 1, :])
                    g.tensor_scalar(ss[:, :, HALF:HD], rot_sb[:, :, 1, :], -1.0, None, ALU.mult)
                    self_.done(g.memset(gain[:], 1.0))
                    for j in range(2):
                        ins = g.tensor_copy(gain[:, j, 0:HEADS], gain_in[:])
                    ins.then_inc(att_consts, 1)
                    for rep in range(REP):
                        for j in range(2):
                            ins = g.tensor_copy(lam_x[:, rep, j, :, :],
                                                lam_in[:].rearrange("p (r i) -> p r i", i=REP)[:, :, rep:rep + 1]
                                                .broadcast_to((P, KVH, HALF)))
                    ins.then_inc(att_consts, 1)

            def power(t):
                wait_apart(pool, stats_done, t + 1, passed)
                self_.done(g.tensor_scalar(rstd[:], mv[:, :, 1], LN_EPS, 1.0, ALU.add, ALU.mult))
                g.tensor_tensor(rstd[:], rstd[:], minus_half[:, 0:SUB], ALU.pow).then_inc(rstd_done, 1)

            def scale(t, par, k):
                pool.wait_ge(wtok_done, t + 1)
                wait_apart(pool, xwT_done, t * E + k - 2, passed)
                for j in range(SUB):
                    ins = g.tensor_scalar(xw[:, k % 2, j, :], xn[:, par, j, :], w_tok[:, par, j, k - 1:k], 1.0,
                                          ALU.mult, ALU.mult)
                ins.then_inc(xw_done, 1)

            def scale_first(t, par, k):
                wait_apart(pool, wtok_done, t + 1, passed)
                for j in range(SUB):
                    ins = g.tensor_scalar(xw[:, k % 2, j, :], xn[:, par, j, :], w_tok[:, par, j, k - 1:k], 1.0,
                                          ALU.mult, ALU.mult)
                ins.then_inc(xw_done, 1)

            def step(t, n, par, first, last):
                if n % 2 == 0 and 3 <= n // 2 + 2 <= E:
                    scale(t, par, n // 2 + 2)

            def prep_at(stage):
                def prep(t, par, n):
                    if n == 4:
                        power(t)
                    if n == 17:
                        for k in (1, 2):
                            (scale_first if isinstance(t, int) and t == 0 else scale)(t, par, k)
                return prep

            def piece(b, p, slot, scores, late, tail, ahead):
                if ahead and slot == 2:
                    wait_apart(pool, a_stats, b + 2, passed)
                    self_.done(g.tensor_scalar(arstd[:], amv[:, :, 1], LN_EPS, 1.0, ALU.add, ALU.mult))
                    g.tensor_tensor(arstd[:], arstd[:], minus_half[:, 0:2], ALU.pow).then_inc(a_rstd, 1)
                if ahead and slot == 12:
                    wait_apart(pool, a_r0, b + 2, passed)
                    self_.done(g.tensor_scalar(ma[:], ms[:], 1.0 / HD, RMS_EPS, ALU.mult, ALU.add))
                    self_.done(g.tensor_tensor(ma[:], ma[:], r0[:], ALU.mult))
                    self_.done(g.tensor_tensor(ma[:], ma[:], r0[:], ALU.mult), apart=passed)
                    self_.done(g.tensor_scalar(ma[:], ma[:], -0.5, 1.5, ALU.mult, ALU.add))
                    self_.done(g.tensor_tensor(ma[:], ma[:], r0[:], ALU.mult))
                    g.tensor_tensor(rq[:], ma[:], gain[:], ALU.mult).then_inc(a_rq, 1)
                u = slot - T_LAG
                if late and u >= 0:
                    hp, j = u // 6, u % 6
                    wait_apart(pool, exp_done, (b - 1) * UNITS + u + 1, passed)
                    if j < 4:
                        v = pr[:, hp % 2, j, :].rearrange("p (i q) -> p i q", i=2)[:, :, 0:P]
                        pat = [[0, 2], [1, P]]
                    else:
                        v = pr[:, hp % 2, j, :].rearrange("p (i q) -> p i q", i=4)
                        pat = [[0, 4], [1, P]]
                    g.affine_select(out=v, in_=v, compare_op=ALU.is_ge, fill=0.0, base=0,
                                    pattern=pat, channel_multiplier=-1).then_inc(sel_done, 1)

            engine_of[0] = pool
            ffn_stage(0, step, prep_at(0), nothing, nothing, [self_], 2, early)
            pool.wait_ge(att_consts, N_ATT)
            attention(piece, 2 * 6, [self_])
            ffn_stage(1, step, prep_at(1), nothing, nothing, [self_], 2)

        @block.scalar
        def _(act):
            s = nc.scalar
            self_ = Links(act, act_self)
            engine_of[0] = act
            def expert_hi(m):
                n = [ORDER[m] in group for group in GROUPS].index(True)
                act.wait_ge(w_loaded[n], 16 * (2 + len(GROUPS[n])))
                s.copy(w_hi[:, ORDER[m]], w_raw[:, ORDER[m]]).then_inc(w_hi_done, 1)

            def early(n):
                if n == 5:
                    act.wait_ge(gw_loaded, 16)
                    s.copy(gw_hi[:], gw_raw[:]).then_inc(w_hi_done, 1)
                if n in SPLIT_AT:
                    for m in SPLIT_AT[n]:
                        expert_hi(m)
                if n == NCH + LEAD - 1:
                    act.wait_ge(small_loaded, 16 * N_SMALL)
                    s.copy(wa_hi[:], wa_raw[:]).then_inc(w_hi_done, 1)

            def step(t, n, par, first, last):
                c = t * NCH + n
                act.wait_ge(g_done, c + 1)
                if not (isinstance(t, int) and t == 0 and n < 2):
                    act.wait_ge(hid_done, c - 1)
                s.activation(act_g[:, n % 2, :], g_ps[n % 2][:], ACT.Silu).then_inc(silu_done, 1)
                if not (first and n == 0):
                    top(t, n - 1)
                if n % 2 == 0 and n // 2 + 1 <= E:
                    k = n // 2 + 1
                    act.wait_ge(xwT_done, t * E + k)
                    if not (isinstance(t, int) and t == 0 and k < 3):
                        act.wait_ge(u_done, c - 2 if k > 2 else c - 1)
                    s.copy(xw_hi[:, k % 2, :], xw_ps[:]).then_inc(xwhi_done, 1)
                if n == 1 and not first:
                    output(t - 1)

            def top(t, n):
                m = t * NCH + n
                act.wait_ge(hid_done, m + 1)
                if not (isinstance(t, int) and t == 0 and n < 3):
                    act.wait_ge(down_done, m - 2)
                s.copy(h_hi[:, n % 3, :], hid[:, n % 2, :]).then_inc(hhi_done, 1)

            def output(t):
                act.wait_ge(down_done, (t + 1) * NCH)
                s.activation(y_sb[:], y_ps[:], ACT.Copy, scale=0.5).then_inc(y_done, 1)

            def prep(t, par, n):
                if n == 7:
                    act.wait_ge(xnT_done, t + 1)
                    s.copy(x_hi[:, par, :], prep_ps[:]).then_inc(xhi_done, 1)
                if n == 10:
                    act.wait_ge(lsub_done, t + 1)
                    s.activation(th[:], lsub[:], ACT.Tanh, scale=0.5).then_inc(tanh_done, 1)

            def tail(t, par):
                top(t, NCH - 1)
                output(t)

            def piece(b, p, slot, scores, late, tail, ahead):
                if late and slot in (3, 8, 13, 18):
                    hp = (slot - 3) // 5
                    act.wait_ge(q2T_done, (b - 1) * 4 + hp + 1)
                    s.copy(q2[:, hp // 2, 2 * (hp % 2):2 * (hp % 2) + 2, :],
                           qT_ps[:].rearrange("p (i q) -> p i q", i=2)).then_inc(q2_done, 1)
                if ahead and slot == 5:
                    act.wait_ge(a_xnT, b + 2)
                    s.copy(xa_hi[:], a_ps[:, 0:2 * P]).then_inc(a_xhi, 1)
                if ahead and slot == 9:
                    act.wait_ge(a_proj, b + 2)
                    if not (isinstance(b, int) and b == -1):
                        act.wait_ge(a_stack, 2 * b + 2)
                        act.wait_ge(a_v, b + 1)
                    pj = a_ps[:, 0:2 * QKV].rearrange("p (j c) -> p j c", j=2)
                    s.copy(qkv[:], pj).then_inc(a_qkv, 1)
                    s.activation(eg[:], pj[:, :, QKV - KVH * HD:QKV], ACT.Exp, scale=-1.0).then_inc(a_eg, 1)
                if ahead and slot == 11:
                    act.wait_ge(a_ms, b + 2)
                    self_.done(s.activation(lnm[:], ms[:], ACT.Ln, bias=eps_col[:], scale=1.0 / HD))
                    s.activation(r0[:], lnm[:], ACT.Exp, scale=-0.5).then_inc(a_r0, 1)
                if ahead and slot == 21:
                    place_keys(b + 1, 1 - p, 0)
                if scores and slot == 0:
                    place_keys(b, p, 1)
                if ahead and slot in (23, 26):
                    place_queries(b + 1, 1 - p, (slot - 23) // 3)
                if scores and slot in (6, 10):
                    place_queries(b, p, 2 + (slot - 6) // 4)
                u = slot - T_LAG
                if late and u >= 0:
                    hp = u // 6
                    act.wait_ge(t_done, (b - 1) * UNITS + u + 1)
                    if u % 6 == 0 and not (isinstance(b, int) and b == 1 and hp < 2):
                        act.wait_ge(pv_done, (b - 1) * 4 + hp - 1)
                    s.activation(pr[:, hp % 2, u % 6, :], t_ps[u % 2][:], ACT.Exp, scale=float(HALF) ** -0.5)\
                        .then_inc(exp_done, 1)
                if late and slot in (14, 20, 26):
                    outputs((b - 1) * 4 + (slot - 14) // 6, (slot - 14) // 6, isinstance(b, int) and b == 1)
                if tail and slot == 4:
                    outputs((b - 2) * 4 + 3, 3, False)
                if tail and slot == 10:
                    act.wait_ge(yaT_done, b - 1)
                    s.copy(ya_hi[:], e_ps[:, 0:2 * P]).then_inc(yahi_done, 1)

            def place_queries(b, p, hp):
                act.wait_ge(a_q1T, b * 4 + hp + 1)
                s.copy(q1[:, p, hp // 2, 2 * (hp % 2):2 * (hp % 2) + 2, :],
                       qT_ps[:].rearrange("p (i q) -> p i q", i=2)).then_inc(a_q1, 1)

            def place_keys(b, p, half):
                act.wait_ge(a_kT, 2 * b + half + 1)
                if not (isinstance(b, int) and b < 2):
                    act.wait_ge(t_done, (b - 2) * UNITS + (half + 1) * UNITS // 2)
                for r in range(KVH):
                    rows = slice(GRP * r, GRP * r + GRP)
                    ins = s.copy(kb[rows, p, half, r, :], a_ps[rows, half * 256:half * 256 + 256])
                ins.then_inc(a_kb, 1)

            def outputs(count, hp, fresh):
                act.wait_ge(pv_done, count + 1)
                if not (fresh and hp < 2):
                    act.wait_ge(oT_done, count - 1)
                s.copy(o_sb[:, hp % 2, :], o_ps[:]).then_inc(o_done, 1)

            ffn_stage(0, step, prep, nothing, tail, early=early)
            act.wait_ge(att_consts, N_ATT)
            act.preload_act_table_set("natural_log_exp_and_others")
            attention(piece, 2, [self_])
            ffn_stage(1, step, prep, nothing, tail)

        @block.vector
        def _(dve):
            v = nc.vector
            engine_of[0] = dve
            self_ = Links(dve, dve_self)

            def early(n):
                if n == 5:
                    dve.wait_ge(w_hi_done, 1)
                    v.tensor_tensor(gw_lo[:], gw_raw[:], gw_hi[:].bitcast(F32), ALU.subtract).then_inc(w_lo_done, 1)
                if n == 9:
                    dve.wait_ge(consts, N_CONST)
                if n in SPLIT_AT:
                    for m in SPLIT_AT[n]:
                        e = ORDER[m]
                        dve.wait_ge(w_hi_done, m + 2)
                        v.tensor_tensor(w_lo[:, e], w_raw[:, e], w_hi[:, e].bitcast(F32), ALU.subtract).then_inc(w_lo_done, 1)
                if n == NCH + LEAD - 1:
                    dve.wait_ge(w_hi_done, E + 3)
                    v.tensor_tensor(wa_lo[:], wa_raw[:], wa_hi[:].bitcast(F32), ALU.subtract).then_inc(w_lo_done, 1)

            def step(t, n, par, first, last):
                c = t * NCH + n
                dve.wait_ge(silu_done, c + 1)
                dve.wait_ge(u_done, c + 1)
                if not (isinstance(t, int) and t == 0 and n < 2):
                    dve.wait_ge(hlo_done, c - 1)
                v.tensor_tensor(hid[:, n % 2, :], act_g[:, n % 2, :], u_ps[n % 2][:], ALU.mult).then_inc(hid_done, 1)
                if not (first and n == 0):
                    rest(t, n - 1)
                if n % 2 == 0 and n // 2 + 1 <= E:
                    k = n // 2 + 1
                    dve.wait_ge(xwhi_done, t * E + k)
                    v.tensor_tensor(xw_lo[:, k % 2, :], xw_ps[:], xw_hi[:, k % 2, :].bitcast(F32),
                                    ALU.subtract).then_inc(xwlo_done, 1)

            def rest(t, n):
                dve.wait_ge(hhi_done, t * NCH + n + 1)
                v.tensor_tensor(h_lo[:, n % 3, :], hid[:, n % 2, :], h_hi[:, n % 3, :].bitcast(F32),
                                ALU.subtract).then_inc(hlo_done, 1)

            def prep_at(stage):
                def prep(t, par, n):
                    tl = t - stage * NT
                    if n == 4:
                        if stage == 0:
                            dve.wait_ge(x_loaded, tl * 16 + 16)
                        for j in range(SUB):
                            ins = v.bn_stats(st[:, j, :], x_sb[:, bass.ds(tl * SUB + j, 1), :].rearrange("p a d -> p (a d)"))
                        self_.done(ins, apart=passed)
                        for j in range(SUB):
                            ins = v.bn_aggr(mv[:, j, :], st[:, j, :])
                        ins.then_inc(stats_done, 1)
                    if n == 5:
                        dve.wait_ge(rstd_done, t + 1)
                        for j in range(SUB):
                            ins = v.tensor_scalar(xn[:, par, j, :],
                                                  x_sb[:, bass.ds(tl * SUB + j, 1), :].rearrange("p a d -> p (a d)"),
                                                  mv[:, j, 0:1], rstd[:, j:j + 1], ALU.subtract, ALU.mult)
                        ins.then_inc(xn_done, 1)
                    if n == 7:
                        dve.wait_ge(xhi_done, t + 1)
                        v.tensor_tensor(x_lo[:, par, :], prep_ps[:], x_hi[:, par, :].bitcast(F32),
                                        ALU.subtract).then_inc(xlo_done, 1)
                    if n == 9:
                        dve.wait_ge(logits_done, t + 1)
                        lg = fin_ps[:, 0:SUB * E].rearrange("p (j e) -> p j e", j=SUB)
                        self_.done(v.tensor_reduce(lmax[:], lg, AX.X, ALU.max))
                        v.tensor_tensor(lsub[:], lg, lmax[:].rearrange("p (j a) -> p j a", a=1).broadcast_to((P, SUB, E)),
                                        ALU.subtract).then_inc(lsub_done, 1)
                    if 10 <= n <= 16:
                        gate(t, par, n - 10)
                return prep

            def gate(t, par, part):
                pj = [lsub[:, j:j + 1, :].broadcast_to((P, E, E)) for j in range(SUB)]
                pe_ = [lsub[:, j, :].rearrange("p (e a) -> p e a", a=1).broadcast_to((P, E, E)) for j in range(SUB)]
                flat = lambda a: a[:].rearrange("p j e f -> p j (e f)")
                over = lambda a: a[:].rearrange("p (o e) f -> p o (e f)", o=1).broadcast_to((P, SUB, E * E))
                if part == 0:
                    dve.wait_ge(lsub_done, t + 1)
                    for j in range(SUB):
                        v.tensor_tensor(cmp_ge[:, j], pj[j], pe_[j], ALU.is_ge)
                if part == 1:
                    for j in range(SUB):
                        ins = v.tensor_tensor(cmp_gt[:, j], pj[j], pe_[j], ALU.is_gt)
                    self_.done(ins)
                if part == 2:
                    v.tensor_tensor(flat(cmp_ge), flat(cmp_ge), over(before), ALU.mult)
                    self_.done(v.tensor_tensor(flat(cmp_gt), flat(cmp_gt), over(after), ALU.mult))
                if part == 3:
                    self_.done(v.tensor_tensor(flat(cmp_ge), flat(cmp_ge), flat(cmp_gt), ALU.add))
                    v.tensor_reduce(rank[:], cmp_ge[:], AX.X, ALU.add)
                if part == 4:
                    dve.wait_ge(tanh_done, t + 1)
                    self_.done(v.tensor_scalar(th1[:], th[:], -1.0, 1.0, ALU.mult, ALU.add))
                    self_.done(v.reciprocal(th1[:], th1[:]))
                    self_.done(v.scalar_tensor_tensor(out=prob[:], in0=th[:], scalar=1.0, in1=th1[:],
                                                      op0=ALU.add, op1=ALU.mult))
                if part == 5:
                    if not (isinstance(t, int) and t == 0):
                        dve.wait_ge(wtok_done, t)
                    v.tensor_reduce(total[:], prob[:], AX.X, ALU.add)
                    self_.done(v.scalar_tensor_tensor(out=chosen[:], in0=rank[:], scalar=2.0, in1=prob[:],
                                                      op0=ALU.is_lt, op1=ALU.mult))
                    self_.done(v.tensor_reduce(top2[:], chosen[:], AX.X, ALU.add))
                if part == 6:
                    self_.done(v.scalar_tensor_tensor(out=top2[:], in0=total[:], scalar=1e-20, in1=top2[:],
                                                      op0=ALU.mult, op1=ALU.add))
                    self_.done(v.reciprocal(rtop[:], top2[:]))
                    v.tensor_tensor(w_tok[:, par], chosen[:],
                                    rtop[:].rearrange("p (j a) -> p j a", a=1).broadcast_to((P, SUB, E)),
                                    ALU.mult).then_inc(wtok_done, 1)

            def finish_at(stage):
                def finish(t, par, last):
                    tl = t - stage * NT
                    dve.wait_ge(yT_done, t + 1)
                    xs = x_sb[:, bass.ds(tl * SUB, SUB), :].rearrange("p j d -> p (j d)")
                    v.tensor_tensor(xs, xs, fin_ps[:], ALU.add).then_inc(xnew_done, 1)
                return finish

            def tail(t, par):
                rest(t, NCH - 1)

            def piece(b, p, slot, scores, late, tail, ahead):
                if late and slot == 0:
                    maxima(b - 1, 1 - p)
                if ahead:
                    project(b + 1, 1 - p, slot)
                if scores and slot == 4:
                    gated_values(b, p)
                if scores and slot == 0 and not (isinstance(b, int) and b == 0):
                    dve.wait_ge(m_done, b)
                if scores and slot in S_SLOT:
                    n = S_SLOT[slot]
                    half, rep, c = S_UNITS[n]
                    dve.wait_ge(s_done, b * UNITS + n + 1)
                    v.tensor_reduce(mx[:, c, half, rep, :], s_ps[n % 2][:].rearrange("p (r k) -> p r k", r=KVH),
                                    AX.X, ALU.max).then_inc(max_done, 1)
                if late and slot in (17, 23):
                    normalise((b - 1) * 4 + (slot - 17) // 6, (slot - 17) // 6)
                if tail and slot == 1:
                    normalise((b - 2) * 4 + 2, 2)
                if tail and slot == 7:
                    normalise((b - 2) * 4 + 3, 3)
                if tail and slot == 8:
                    combine(b - 2)
                if tail and slot == 11:
                    dve.wait_ge(yahi_done, b - 1)
                    v.tensor_tensor(ya_lo[:], e_ps[:, 0:2 * P], ya_hi[:].bitcast(F32), ALU.subtract).then_inc(yalo_done, 1)
                if tail and slot == 13:
                    dve.wait_ge(wo_done, b - 1)
                    xs = x_sb[:, bass.ds((b - 2) * 2, 2), :].rearrange("p j d -> p (j d)")
                    v.tensor_tensor(xs, xs, e_ps[:, 2 * P:4 * P], ALU.add).then_inc(att_done, 1)

            def gated_values(b, p):
                dve.wait_ge(a_eg, b + 1)
                if not (isinstance(b, int) and b < 2):
                    dve.wait_ge(pv_done, (b - 1) * 4)
                self_.done(v.tensor_scalar(eg[:], eg[:], 1.0, None, ALU.add))
                self_.done(v.reciprocal(eg[:], eg[:]))
                for j in range(2):
                    vv = qkv[:, j, NH * HD:NH * HD + KVH * HD].rearrange("p (r d) -> p r d", r=KVH)
                    gg = eg[:, j, :].rearrange("p (r d) -> p r d", r=KVH)
                    for half in range(2):
                        d = slice(HALF * half, HALF * half + HALF)
                        ins = v.tensor_tensor(v1[:, p, j, half, :, 0:HALF], vv[:, :, d], gg[:, :, d], ALU.mult)
                ins.then_inc(a_v, 1)

            def maxima(b, p):
                dve.wait_ge(max_done, (b + 1) * UNITS)
                flat = mx[:].rearrange("p c h i r -> p c (h i r)")
                self_.done(v.tensor_tensor(flat[:, 1, :], flat[:, 1, :], flat[:, 2, :], ALU.max))
                m = flat[:, 0:2, :].rearrange("p c g -> p (c g)")
                st_ = qs[:, p].rearrange("p j h i r c -> p (j h i r) c")
                self_.done(v.tensor_scalar(st_[:, :, 12].bitcast(F32R), m, -1.0, None, ALU.mult))
                v.scalar_tensor_tensor(out=st_[:, :, 13], in0=m, scalar=-1.0, in1=st_[:, :, 12],
                                       op0=ALU.mult, op1=ALU.subtract).then_inc(m_done, 1)

            def project(b, p, slot):
                if slot == 1:
                    for j in range(2):
                        ins = v.bn_stats(ast[:, j, :], x_sb[:, bass.ds(b * 2 + j, 1), :].rearrange("p a d -> p (a d)"))
                    self_.done(ins, apart=passed)
                    for j in range(2):
                        ins = v.bn_aggr(amv[:, j, :], ast[:, j, :])
                    ins.then_inc(a_stats, 1)
                if slot == 3:
                    dve.wait_ge(a_rstd, b + 1)
                    for j in range(2):
                        ins = v.tensor_scalar(xa[:, j, :], x_sb[:, bass.ds(b * 2 + j, 1), :].rearrange("p a d -> p (a d)"),
                                              amv[:, j, 0:1], arstd[:, j:j + 1], ALU.subtract, ALU.mult)
                    ins.then_inc(a_xn, 1)
                if slot == 6:
                    dve.wait_ge(a_xhi, b + 1)
                    v.tensor_tensor(xa_lo[:], a_ps[:, 0:2 * P], xa_hi[:].bitcast(F32), ALU.subtract).then_inc(a_xlo, 1)
                qk = qkv[:, :, 0:NH * HD].rearrange("p j (h d) -> p j h d", h=NH)
                if slot == 10:
                    dve.wait_ge(a_qkv, b + 1)
                    self_.done(v.tensor_tensor(sq[:].rearrange("p j h d -> p j (h d)"), qkv[:, :, 0:NH * HD],
                                               qkv[:, :, 0:NH * HD], ALU.mult))
                    v.tensor_reduce(ms[:], sq[:], AX.X, ALU.add).then_inc(a_ms, 1)
                if slot == 14:
                    dve.wait_ge(a_rq, b + 1)
                    if not (isinstance(b, int) and b == 0):
                        dve.wait_ge(a_stack, 2 * b)
                    for j in range(2):
                        ins = v.tensor_tensor(qn[:, j], qk[:, j],
                                              rq[:, j, :].rearrange("p (h a) -> p h a", a=1).broadcast_to((P, NH, HD)),
                                              ALU.mult)
                    self_.done(ins)
                if slot in (15, 16):
                    j = slot - 15
                    one = lambda a, n: a.rearrange("p (a d) -> p a d", a=1).broadcast_to((P, NH, n))
                    v.tensor_tensor(ra[:, j], qn[:, j], one(cc[:, j, :], HD), ALU.mult)
                    v.tensor_tensor(rb[:, j, :, 0:HALF], qn[:, j, :, HALF:HD], one(ss[:, j, 0:HALF], HALF), ALU.mult)
                    ins = v.tensor_tensor(rb[:, j, :, HALF:HD], qn[:, j, :, 0:HALF], one(ss[:, j, HALF:HD], HALF), ALU.mult)
                    if j == 1:
                        self_.done(ins)
                if slot == 17:
                    self_.done(v.tensor_tensor(ra[:].rearrange("p j h d -> p (j h d)"), ra[:].rearrange("p j h d -> p (j h d)"),
                                               rb[:].rearrange("p j h d -> p (j h d)"), ALU.add))
                if slot in (18, 19, 21, 23):
                    half, j = divmod((18, 19, 21, 23).index(slot), 2)
                    if slot == 18:
                        if not (isinstance(b, int) and b == 0):
                            dve.wait_ge(a_kT, 2 * b)
                        if not (isinstance(b, int) and b < 2):
                            dve.wait_ge(q2T_done, (b - 1) * 4)
                        st_ = qs[:, p].rearrange("p j h i r c -> p (j h i r) c")
                        v.memset(st_[:, :, 12:14], 0.0)
                    d = slice(HALF * half, HALF * half + HALF)
                    rq_ = ra[:, j, 0:HEADS].rearrange("p (r i) d -> p i r d", i=REP)[:, :, :, d]
                    rk_ = ra[:, j, HEADS:NH][:, :, d]
                    qs_, ks_ = qs[:, p, j, half], ks[:, j, half]
                    v.tensor_copy(qs_[:, :, :, 0:4].bitcast(F32R), rq_)
                    v.tensor_copy(qs_[:, :, :, 4:8].bitcast(F32R), rq_)
                    v.tensor_copy(ks_[:, :, 0:4].bitcast(F32R), rk_)
                    self_.done(v.tensor_copy(ks_[:, :, 8:12].bitcast(F32R), rk_))
                    v.tensor_tensor(qs_[:, :, :, 8:12], rq_, qs_[:, :, :, 0:4], ALU.subtract)
                    ins = v.tensor_tensor(ks_[:, :, 4:8], rk_, ks_[:, :, 0:4], ALU.subtract)
                    if j == 1:
                        ins.then_inc(a_stack, 1)

            def normalise(count, hp):
                dve.wait_ge(oT_done, count + 1)
                o = e_ps[:].rearrange("p (g c) -> p g c", c=GRP)
                self_.done(v.reciprocal(rden[:], o[:, :, HALF]))
                v.tensor_tensor(an[:, hp // 2, hp % 2], o[:, :, 0:HALF],
                                rden[:].rearrange("p (g a) -> p g a", a=1).broadcast_to((P, 16, HALF)),
                                ALU.mult).then_inc(an_done, 1)

            def combine(b):
                dve.wait_ge(an_done, (b + 1) * 4)
                flat = an[:].rearrange("p h i g d -> p h (i g d)")
                self_.done(v.tensor_tensor(lt[:], flat[:, 1, :], lam_x[:].rearrange("p i j r d -> p (i j r d)"), ALU.mult))
                a1 = flat[:, 0, :].rearrange("p (i j r d) -> p j i r d", i=REP, j=2, r=KVH)
                l2 = lt[:].rearrange("p (i j r d) -> p j i r d", i=REP, j=2, r=KVH)
                for j in range(2):
                    yo = ya[:, j].rearrange("p (r i) d -> p i r d", i=REP)
                    v.tensor_tensor(yo[:, :, :, 0:HALF], a1[:, j], l2[:, j], ALU.subtract)
                    ins = v.tensor_tensor(yo[:, :, :, HALF:HD], a1[:, j], l2[:, j], ALU.add)
                ins.then_inc(ya_done, 1)

            ffn_stage(0, step, prep_at(0), finish_at(0), tail, [self_], 2 * DVE_FFN, early)
            dve.wait_ge(att_consts, N_ATT)
            attention(piece, 2 * DVE_ATT, [self_])
            dve.wait_ge(att_done, BATCH)
            ffn_stage(1, step, prep_at(1), finish_at(1), tail, [self_], 2 * DVE_FFN)

        @block.tensor
        def _(pe):
            t_ = nc.tensor
            engine_of[0] = pe
            pe.wait_ge(consts, N_CONST)

            def product(o, w_h, w_l, m_h, m_l, start=True, stop=True):
                t_.matmul(o, w_h, m_h, start=start, stop=False)
                t_.matmul(o, w_l, m_h, start=False, stop=False)
                return t_.matmul(o, w_h, m_l, start=False, stop=stop)

            def step(t, n, par, first, last):
                c = t * NCH + n
                e, h = ORDER[n // 2], (n % 2) * P
                zero = isinstance(t, int) and t == 0
                if n % 2 == 0:
                    pe.wait_ge(w_lo_done, expert_lo(n // 2))
                if n == 0:
                    pe.wait_ge(xhi_done, t + 1)
                    pe.wait_ge(xlo_done, t + 1)
                if not (zero and n < 2):
                    pe.wait_ge(silu_done, c - 1)
                product(g_ps[n % 2][:], w_hi[:, e, 0, h:h + P], w_lo[:, e, 0, h:h + P],
                        x_hi[:, par, :], x_lo[:, par, :]).then_inc(g_done, 1)
                if not (zero and n < 2):
                    pe.wait_ge(hid_done, c - 1)
                k = n // 2
                if k:
                    pe.wait_ge(xwhi_done, t * E + k)
                    pe.wait_ge(xwlo_done, t * E + k)
                    mh, ml = xw_hi[:, k % 2, :], xw_lo[:, k % 2, :]
                else:
                    mh, ml = x_hi[:, par, :], x_lo[:, par, :]
                product(u_ps[n % 2][:], w_hi[:, e, 1, h:h + P], w_lo[:, e, 1, h:h + P], mh, ml).then_inc(u_done, 1)
                if n % 2 == 0 and n // 2 + 1 <= E:
                    k = n // 2 + 1
                    pe.wait_ge(xw_done, t * E + k)
                    if not (zero and k == 1):
                        pe.wait_ge(xwlo_done, t * E + k - 1)
                    for j in range(SUB):
                        ins = t_.transpose(xw_ps[:, j * P:(j + 1) * P], xw[:, k % 2, j, :], ident[:])
                    ins.then_inc(xwT_done, 1)
                if n >= 2 or not first:
                    down(t, n - 2) if n >= 2 else down(t - 1, n - 2 + NCH)

            def down(t, n):
                c = t * NCH + n
                e, q = ORDER[n // 2], (n % 2) * P
                pe.wait_ge(hhi_done, c + 1)
                pe.wait_ge(hlo_done, c + 1)
                if n == 0 and not (isinstance(t, int) and t == 0):
                    pe.wait_ge(y_done, t)
                product(y_ps[:], w_hi[:, e, 2, q:q + P], w_lo[:, e, 2, q:q + P], h_hi[:, n % 3, :], h_lo[:, n % 3, :],
                        start=n == 0, stop=n == NCH - 1).then_inc(down_done, 1)

            def prep(t, par, n):
                if n == 6:
                    pe.wait_ge(xn_done, t + 1)
                    for j in range(SUB):
                        ins = t_.transpose(prep_ps[:, j * P:(j + 1) * P], xn[:, par, j, :], ident[:])
                    ins.then_inc(xnT_done, 1)
                if n == 8:
                    pe.wait_ge(xhi_done, t + 1)
                    pe.wait_ge(xlo_done, t + 1)
                    if isinstance(t, int) and t == 0:
                        pe.wait_ge(w_lo_done, 1)
                    for j in range(SUB):
                        q = slice(j * P, (j + 1) * P)
                        ins = product(fin_ps[:, j * E:(j + 1) * E], x_hi[:, par, q], x_lo[:, par, q], gw_hi[:], gw_lo[:])
                    ins.then_inc(logits_done, 1)

            def tail(t, par):
                down(t, NCH - 2)
                down(t, NCH - 1)

            def finish(t, par, last):
                pe.wait_ge(y_done, t + 1)
                pe.wait_ge(lsub_done, t + 1 if last else t + 2)
                for j in range(SUB):
                    ins = t_.transpose(fin_ps[:, j * P:(j + 1) * P], y_sb[:, j * P:(j + 1) * P], ident[:])
                ins.then_inc(yT_done, 1)

            def piece(b, p, slot, scores, late, tail, ahead):
                if scores and slot in S_SLOT:
                    n = S_SLOT[slot]
                    half, rep, c = S_UNITS[n]
                    qt, kt, edge = COMBOS[c]
                    pe.wait_ge(a_q1, b * 4 + half * 2 + rep // 2 + 1)
                    pe.wait_ge(a_kb, b * 2 + half + 1)
                    if not (isinstance(b, int) and b == 0 and n < 2):
                        pe.wait_ge(max_done, b * UNITS + n - 1)
                    o = s_ps[n % 2][:].rearrange("p (r k) -> p r k", r=KVH)
                    if edge:
                        t_.matmul(o, ident_b[:], mask_b[:], start=True, stop=False)
                    t_.matmul(o, q1[:, p, half, rep, qt * P:(qt + 1) * P], kb[:, p, half, :, kt * P:(kt + 1) * P],
                              start=not edge, stop=True).then_inc(s_done, 1)
                u = slot - T_LAG
                if late and u >= 0:
                    hp, j = u // 6, u % 6
                    half, i0 = hp // 2, 2 * (hp % 2)
                    if j == 0:
                        pe.wait_ge(q2_done, (b - 1) * 4 + hp + 1)
                    if not (isinstance(b, int) and b == 1 and u < 2):
                        pe.wait_ge(exp_done, (b - 1) * UNITS + u - 1)
                    if j < 4:
                        ins = t_.matmul(t_ps[u % 2][:], kb[:, 1 - p, half, j, 0:P], q2[:, half, i0:i0 + 2, :],
                                        start=True, stop=True)
                    else:
                        for r in (2 * (j - 4), 2 * (j - 4) + 1):
                            ins = t_.matmul(t_ps[u % 2][:, (r % 2) * 256:(r % 2) * 256 + 256],
                                            kb[:, 1 - p, half, r, P:2 * P], q2[:, half, i0:i0 + 2, P:2 * P],
                                            start=True, stop=True)
                    ins.then_inc(t_done, 1)
                if late and slot in (2, 7, 12, 17):
                    hp = (slot - 2) // 5
                    pe.wait_ge(m_done, b)
                    if hp == 3:
                        pe.wait_ge(q2_done, (b - 1) * 4 + 3)
                    else:
                        pe.wait_ge(a_q1, b * 4 + 2 + hp if scores else BATCH * 4)
                    if hp == 1 and not scores:
                        pe.wait_ge(q2_done, (b - 1) * 4 + 1)
                    if hp == 2 and not scores:
                        pe.wait_ge(q2_done, (b - 1) * 4 + 2)
                    turn_queries(1 - p, hp).then_inc(q2T_done, 1)
                if scores and slot in (5, 9):
                    hp = 2 + (slot - 5) // 4
                    pe.wait_ge(a_stack, 2 * b + 2)
                    if late:
                        pe.wait_ge(q2_done, (b - 1) * 4 + hp - 1)
                    else:
                        pe.wait_ge(a_q1, b * 4 + hp)
                    turn_queries(p, hp).then_inc(a_q1T, 1)
                if ahead:
                    project(b + 1, 1 - p, slot, late)
                if late and slot in (12, 13, 18, 19, 24, 25):
                    values(b - 1, (slot - 12) // 6, slot % 2, 1 - p, isinstance(b, int) and b == 1)
                if late and slot in (16, 22):
                    turn_outputs((b - 1) * 4 + (slot - 16) // 6, (slot - 16) // 6, isinstance(b, int) and b == 1, b)
                if tail and slot == 0:
                    turn_outputs((b - 2) * 4 + 2, 2, False, b)
                if tail and slot in (2, 3):
                    values(b - 2, 3, slot % 2, p, False)
                if tail and slot == 6:
                    turn_outputs((b - 2) * 4 + 3, 3, False, b)
                if tail and slot == 9:
                    pe.wait_ge(ya_done, b - 1)
                    pe.wait_ge(an_done, (b - 1) * 4)
                    for j in range(2):
                        ins = t_.transpose(e_ps[:, j * P:(j + 1) * P], ya[:, j].rearrange("p h d -> p (h d)"), ident[:])
                    ins.then_inc(yaT_done, 1)
                if tail and slot == 12:
                    pe.wait_ge(yahi_done, b - 1)
                    pe.wait_ge(yalo_done, b - 1)
                    for j in range(2):
                        q = slice(j * P, (j + 1) * P)
                        ins = product(e_ps[:, (2 + j) * P:(3 + j) * P], ya_hi[:, q], ya_lo[:, q], wa_hi[:, QKV:], wa_lo[:, QKV:])
                    ins.then_inc(wo_done, 1)

            def turn_queries(p, hp):
                half, i0 = hp // 2, 2 * (hp % 2)
                for i in range(2):
                    for j in range(2):
                        o = (2 * i + j) * P
                        ins = t_.transpose(qT_ps[:, o:o + P], qs[:, p, j, half, i0 + i].rearrange("p r c -> p (r c)"), ident[:])
                return ins

            def project(b, p, slot, late):
                if slot == 4:
                    pe.wait_ge(a_xn, b + 1)
                    if not (isinstance(b, int) and b == 0):
                        pe.wait_ge(a_kb, b * 2)
                    for j in range(2):
                        ins = t_.transpose(a_ps[:, j * P:(j + 1) * P], xa[:, j, :], ident[:])
                    ins.then_inc(a_xnT, 1)
                if slot == 8:
                    pe.wait_ge(a_xhi, b + 1)
                    pe.wait_ge(a_xlo, b + 1)
                    for j in range(2):
                        q = slice(j * P, (j + 1) * P)
                        ins = product(a_ps[:, j * QKV:(j + 1) * QKV], xa_hi[:, q], xa_lo[:, q], wa_hi[:, 0:QKV], wa_lo[:, 0:QKV])
                    ins.then_inc(a_proj, 1)
                if slot in (20, 24):
                    half = (slot - 20) // 4
                    pe.wait_ge(a_stack, 2 * b + half + 1)
                    if half:
                        pe.wait_ge(a_kb, 2 * b + 1)
                    else:
                        pe.wait_ge(a_eg, b + 1)
                    for j in range(2):
                        o = (2 * half + j) * P
                        ins = t_.transpose(a_ps[:, o:o + P], ks[:, j, half].rearrange("p r c -> p (r c)"), ident[:])
                    ins.then_inc(a_kT, 1)
                if slot in (22, 25):
                    hp = (slot - 22) // 3
                    pe.wait_ge(a_stack, 2 * b + 1)
                    if hp == 0 and late:
                        pe.wait_ge(q2_done, (b - 1) * 4)
                    elif not (isinstance(b, int) and b == 0 and hp == 0):
                        pe.wait_ge(a_q1, b * 4 + hp)
                    turn_queries(p, hp).then_inc(a_q1T, 1)

            def values(batch, hp, kt, p, fresh):
                count, half = batch * 4 + hp, hp // 2
                if kt == 0:
                    pe.wait_ge(sel_done, count * 6 + 4)
                    pe.wait_ge(a_v, batch + 1)
                    if not (fresh and hp == 0):
                        pe.wait_ge(o_done, count)
                    for r in range(KVH):
                        t_.matmul(o_ps[GRP * r:GRP * r + GRP, :], v1[:, p, 0, half, r, :], pr[:, hp % 2, r, :],
                                  start=True, stop=False)
                else:
                    pe.wait_ge(sel_done, (count + 1) * 6)
                    for r in range(KVH):
                        ins = t_.matmul(o_ps[GRP * r:GRP * r + GRP, :].rearrange("p (i q) -> p i q", i=2)[:, :, P:2 * P],
                                        v1[:, p, 1, half, r, :],
                                        pr[:, hp % 2, 4 + r // 2, (r % 2) * 256:(r % 2) * 256 + 256].rearrange("p (i q) -> p i q", i=2),
                                        start=False, stop=True)
                    ins.then_inc(pv_done, 1)

            def turn_outputs(count, hp, fresh, b):
                pe.wait_ge(o_done, count + 1)
                if not (fresh and hp == 0):
                    pe.wait_ge(an_done, count)
                if hp == 0 and not fresh and not (isinstance(b, int) and b < 2):
                    pe.wait_ge(att_done, b - 1)
                for i in range(4):
                    ins = t_.transpose(e_ps[:, i * P:(i + 1) * P], o_sb[:, hp % 2, i * P:(i + 1) * P], ident[:])
                ins.then_inc(oT_done, 1)

            ffn_stage(0, step, prep, finish, tail)
            pe.wait_ge(xnew_done, NT)
            pe.wait_ge(xwlo_done, NT * E)
            pe.wait_ge(att_consts, N_ATT)
            pe.wait_ge(w_lo_done, expert_lo(E + 1))
            attention(piece)
            pe.wait_ge(att_done, BATCH)
            pe.wait_ge(a_kb, 2 * BATCH)
            pe.wait_ge(exp_done, BATCH * UNITS)
            pe.wait_ge(max_done, BATCH * UNITS)
            ffn_stage(1, step, prep, finish, tail)


DVE_FFN = 12
DVE_ATT = 18



def kernel(**inputs):
    import numpy as np
    import concourse.bacc as bacc
    from concourse.bass_utils import run_bass_kernel_spmd

    g = {k: np.asarray(v) for k, v in inputs.items()}
    angles = np.arange(0, HD, 2, dtype=np.float32) / np.float32(HD) * np.float32(np.pi)
    pos = np.arange(SEQ, dtype=np.float32)
    radius = np.float32(1.0) / (np.float32(1.0) + pos[:, None] * np.float32(0.01))
    ang = (pos[:, None] * angles[None, :]).astype(np.float32)
    rot = np.stack([radius * np.cos(ang.astype(np.float64)).astype(np.float32),
                    radius * np.sin(ang.astype(np.float64)).astype(np.float32)], axis=1).astype(np.float32)
    send = {
        "x": g["L0_attn_x"], "w_gate": g["L0_ffn_w_gate"], "w_up": g["L0_ffn_w_up"], "w_down": g["L0_ffn_w_down"],
        "ws_gate": g["L0_ffn_ws_gate"], "ws_up": g["L0_ffn_ws_up"], "ws_down": g["L0_ffn_ws_down"],
        "gate_w": g["L0_ffn_gate_w"],
        "wqkv": np.concatenate([g["L0_attn_Wq"], g["L0_attn_Wk"], g["L0_attn_Wv"], g["L0_attn_Wg"]], axis=0).T,
        "wo": g["L0_attn_Wo"].T, "q_gain": g["L0_attn_q_gain"], "lam": g["L0_attn_lambda_param"], "rot": rot,
    }
    nc = bacc.Bacc("TRN2", target_bir_lowering=False, num_devices=1)
    arrays, args = {}, []
    for name, a in send.items():
        a = np.ascontiguousarray(a)
        arrays[f"in_{name}_dram"] = a
        args.append(nc.dram_tensor(f"in_{name}_dram", a.shape, mybir.dt.from_np(a.dtype), kind="ExternalInput").ap())
    o = nc.dram_tensor("out_0_dram", (BATCH, SEQ, DIM), F32, kind="ExternalOutput").ap()
    macaron(nc, *args, o)
    r = run_bass_kernel_spmd(nc, [arrays], core_ids=[0])
    return r.results[0]["out_0_dram"]
```

```python
from contextlib import ExitStack

import concourse.bass as bass
from concourse import mybir

F32 = mybir.dt.float32
F32R = mybir.dt.float32r
BF16 = mybir.dt.bfloat16
ALU = mybir.AluOpType
ACT = mybir.ActivationFunctionType
AX = mybir.AxisListType

P = 128
BATCH, SEQ, DIM = 16, 256, 128
TOKT = BATCH * SEQ // P
TILE = 512
SUB = TILE // P
NT = BATCH * SEQ // TILE
E, HID = 8, 256
NCH = (E + 1) * 2
LEAD = 4
HEADS, KVH, HD = 16, 4, 8
HALF = HD // 2
REP = HEADS // KVH
QKV = DIM + 3 * KVH * HD
NH = HEADS + KVH
GRP = 32
LN_EPS = 1e-5
RMS_EPS = 1.1920928955078125e-07
NEG = -1.0e30
UNITS = 24
T_LAG = 4
SLOTS = UNITS + T_LAG


class Links:

    def __init__(self, engine, sem):
        self.engine, self.sem, self.base, self.n = engine, sem, 0, 0

    def done(self, ins, apart=None):
        self.n += 1
        ins.then_inc(self.sem, 1)
        if apart:
            wait_apart(self.engine, self.sem, self.base + self.n, apart)
        else:
            self.engine.wait_ge(self.sem, self.base + self.n)

    def enter(self, i, per):
        self.start, self.per = self.base + self.n, per
        self.base, self.n = self.start + i * per, 0

    def leave(self, times):
        assert self.n == self.per, f"{self.n} steps in the body, not {self.per}"
        self.base, self.n = self.start + times * self.per, 0


def wait_apart(engine, sem, value, passed):
    engine.wait_ge(sem, value)
    engine.sem_inc(passed, 1)


def macaron(nc, x_in, w_gate, w_up, w_down, ws_gate, ws_up, ws_down, gate_w, wqkv, wo, q_gain, lam, rot, out):
    ctx = ExitStack()
    with ctx:
        def sb(name, shape, dt=F32):
            return ctx.enter_context(nc.sbuf_tensor(name, shape, dt))

        def sem(name):
            return ctx.enter_context(nc.semaphore(name))

        bank = [ctx.enter_context(nc.psum_tensor(f"bank{i}", [P, 512], F32)) for i in range(8)]
        g_ps, u_ps, y_ps, xw_ps, prep_ps, fin_ps = bank[0:2], bank[2:4], bank[4], bank[5], bank[6], bank[7]
        s_ps, t_ps, o_ps, qT_ps, a_ps, e_ps = bank[0:2], bank[2:4], bank[4], bank[5], bank[6], bank[7]

        x_sb = sb("x_sb", [P, TOKT, DIM])
        w_raw = sb("w_raw", [P, E + 1, 3, HID])
        w_hi = sb("w_hi", [P, E + 1, 3, HID], F32R)
        w_lo = sb("w_lo", [P, E + 1, 3, HID], F32R)
        pr = w_raw[:].rearrange("p e j d -> p (e j d)")[:, 0:6144].rearrange("p (a j n) -> p a j n", a=2, j=6)
        arena = sb("arena", [P, 7168], F32R)

        def cut(at, *dims):
            size = 1
            for d in dims:
                size *= d
            names_ = "abcd"[:len(dims)]
            flat = arena[:, at:at + size]
            return flat.rearrange(f"p ({' '.join(names_)}) -> p {' '.join(names_)}", **dict(zip(names_, dims)))

        gw_raw = sb("gw_raw", [P, E])
        gw_both = sb("gw_both", [P, 2 * E], F32R)
        gw_hi, gw_lo = gw_both[:, 0:E], gw_both[:, E:2 * E]
        wa_raw = sb("wa_raw", [P, QKV + DIM])
        wa_hi, wa_lo = sb("wa_hi", [P, QKV + DIM], F32R), sb("wa_lo", [P, QKV + DIM], F32R)
        ident_r = sb("ident_r", [P, P], F32R)
        ident = ident_r[:].bitcast(F32)
        ident_b = sb("ident_b", [P, P], BF16)
        mask_b = sb("mask_b", [P, KVH, P], BF16)
        minus_half = sb("minus_half", [P, SUB])
        before = sb("before", [P, E, E])
        after = sb("after", [P, E, E])

        st = sb("st", [P, SUB, 6])
        mv = sb("mv", [P, SUB, 2])
        rstd = sb("rstd", [P, SUB])
        xn = sb("xn", [P, 2, SUB, DIM])
        x_hi, x_lo = cut(0, 2, TILE), cut(1024, 2, TILE)
        lmax = sb("lmax", [P, SUB])
        lsub = sb("lsub", [P, SUB, E])
        prob = sb("prob", [P, SUB, E])
        cmp_ge, cmp_gt = sb("cmp_ge", [P, SUB, E, E]), sb("cmp_gt", [P, SUB, E, E])
        rank, chosen = sb("rank", [P, SUB, E]), sb("chosen", [P, SUB, E])
        total, top2, rtop = sb("total", [P, SUB]), sb("top2", [P, SUB]), sb("rtop", [P, SUB])
        w_tok = sb("w_tok", [P, 2, SUB, E])
        xw = sb("xw", [P, 2, SUB, DIM])
        xw_hi, xw_lo = cut(2048, 2, TILE), cut(3072, 2, TILE)
        act_g = sb("act_g", [P, 2, TILE])
        hid = sb("hid", [P, 2, TILE])
        h_hi, h_lo = cut(4096, 3, TILE), cut(5632, 3, TILE)
        y_sb = sb("y_sb", [P, TILE])

        rot_sb = sb("rot_sb", [P, 2, 2, HALF])
        cc = sb("cc", [P, 2, HD])
        ss = sb("ss", [P, 2, HD])
        gain_in = sb("gain_in", [P, HEADS])
        lam_in = sb("lam_in", [P, HEADS])
        gain = sb("gain", [P, 2, NH])
        lam_x = sb("lam_x", [P, REP, 2, KVH, HALF])
        ast, amv, arstd = sb("ast", [P, 2, 6]), sb("amv", [P, 2, 2]), sb("arstd", [P, 2])
        xa = sb("xa", [P, 2, DIM])
        xa_hi, xa_lo = sb("xa_hi", [P, 2 * P], F32R), sb("xa_lo", [P, 2 * P], F32R)
        qkv = sb("qkv", [P, 2, QKV])
        eg = sb("eg", [P, 2, KVH * HD])
        ms = sb("ms", [P, 2, NH])
        ma, r0, lnm = sb("ma", [P, 2, NH]), sb("r0", [P, 2, NH]), sb("lnm", [P, 2, NH])
        rq = sb("rq", [P, 2, NH])
        eps_col = sb("eps_col", [P, 1])
        th, th1 = sb("th", [P, SUB, E]), sb("th1", [P, SUB, E])
        qn = sb("qn", [P, 2, NH, HD])
        ra, rb = sb("ra", [P, 2, NH, HD]), sb("rb", [P, 2, NH, HD])
        sq = rb
        qs = sb("qs", [P, 2, 2, 2, REP, KVH, GRP], F32R)
        ks = sb("ks", [P, 2, 2, KVH, GRP], F32R)
        q1 = cut(0, 2, 2, REP, SEQ)
        q2 = cut(4096, 2, REP, SEQ)
        kb = sb("kb", [P, 2, 2, KVH, SEQ], F32R)
        v1 = sb("v1", [P, 2, 2, 2, KVH, GRP])
        mx = sb("mx", [P, 2, 3, 2, REP, KVH])
        o_sb = act_g
        rden = sb("rden", [P, 16])
        an = sb("an", [P, 2, 2, 16, HALF])
        ya = sb("ya", [P, 2, HEADS, HD])
        lt = sb("lt", [P, P])
        ya_hi, ya_lo = sb("ya_hi", [P, 2 * P], F32R), sb("ya_lo", [P, 2 * P], F32R)

        names = """x_loaded gw_loaded small_loaded x_stored consts att_consts w_hi_done w_lo_done
            stats_done rstd_done xn_done xnT_done xhi_done xlo_done logits_done lsub_done cmp_done beats_done tanh_done
            wtok_done xw_done xwT_done xwhi_done xwlo_done g_done u_done silu_done hid_done hhi_done
            hlo_done down_done y_done yT_done xnew_done dve_self pool_self
            a_stats a_rstd a_xn a_xnT a_xhi a_xlo a_proj a_qkv a_eg a_ms a_r0 a_rq act_self a_sig a_v a_clear a_stack a_kT a_kb
            a_q1T a_q1 s_done max_done m_done q2T_done q2_done t_done exp_done sel_done pv_done
            o_done oT_done an_done ya_done yaT_done yahi_done yalo_done wo_done att_done passed""".split()
        S = {n: sem(n) for n in names}
        (x_loaded, gw_loaded, small_loaded, x_stored, consts, att_consts, w_hi_done, w_lo_done,
         stats_done, rstd_done, xn_done, xnT_done, xhi_done, xlo_done, logits_done, lsub_done, cmp_done, beats_done, tanh_done,
         wtok_done, xw_done, xwT_done, xwhi_done, xwlo_done, g_done, u_done, silu_done, hid_done, hhi_done,
         hlo_done, down_done, y_done, yT_done, xnew_done, dve_self, pool_self,
         a_stats, a_rstd, a_xn, a_xnT, a_xhi, a_xlo, a_proj, a_qkv, a_eg, a_ms, a_r0, a_rq, act_self, a_sig, a_v, a_clear, a_stack, a_kT, a_kb,
         a_q1T, a_q1, s_done, max_done, m_done, q2T_done, q2_done, t_done, exp_done, sel_done, pv_done,
         o_done, oT_done, an_done, ya_done, yaT_done, yahi_done, yalo_done, wo_done, att_done, passed) = [S[n] for n in names]

        GROUPS = [[E], [0], [1, 2], [3, 4], [5, 6, 7]]
        w_loaded = [sem(f"w_loaded{n}") for n in range(len(GROUPS))]

        ORDER = [E] + list(range(E))
        x_tok = x_in.rearrange("b (j p) d -> p (b j) d", p=P)
        out_tok = out.rearrange("b (j p) d -> p (b j) d", p=P)
        N_CONST = 4
        N_ATT = 5
        N_SMALL = 5

        SPLIT_AT = {6: [0], 9: [1], NCH: [2], NCH + 1: [3], NCH + 2: [4], NCH + 3: [5, 6, 7, 8]}

        def expert_lo(m):
            return m + 2

        block = ctx.enter_context(nc.Block())

        def nothing(*a):
            pass

        def ffn_stage(stage, step, prep, finish, tail, links=None, per=0, early=nothing, begun=False, meanwhile=nothing):
            t0 = stage * NT

            def tile(t, par, last):
                for n in range(LEAD, NCH):
                    step(t, n, par, False, last)
                    if not last:
                        prep(t + 1, 1 - par, n)
                    else:
                        meanwhile(n)
                if not last:
                    for n in range(LEAD):
                        step(t + 1, n, 1 - par, False, False)
                    finish(t, par, last)
                else:
                    tail(t, par)
                    finish(t, par, last)

            if not begun:
                for n in range(LEAD, NCH):
                    prep(t0, 0, n)
                    early(n)
                for n in range(LEAD):
                    step(t0, n, 0, True, False)
                    early(NCH + n)
            with (links[0].engine if links else engine_of[0]).Fori(0, NT // 2 - 1) as i:
                if links:
                    for li in links:
                        li.enter(i, per)
                tile(t0 + 2 * i, 0, False)
                tile(t0 + 2 * i + 1, 1, False)
            if links:
                for li in links:
                    li.leave(NT // 2 - 1)
            tile(t0 + NT - 2, 0, False)
            tile(t0 + NT - 1, 1, True)

        engine_of = [None]

        BESIDE = {4: [0, 1], 5: [2, 3], 7: [4], 8: [5], 9: [6, 7], 11: [8, 9, 10], 12: [11], 14: [12, 13, 14], 15: [15, 16],
                  16: [17, 18], 17: [19, 20]}
        FIRST_LEFT = 21

        def start_attention(piece):
            def meanwhile(n):
                for slot in BESIDE.get(n, []):
                    piece(-1, 1, slot, False, False, False, True)
            return meanwhile

        PREP_AFTER = {(0, 4): [4], (0, 8): [5], (0, 10): [6], (0, 12): [7], (0, 14): [8], (0, 15): [9],
                      (0, 27): [10, 11, 12], (1, 0): [13], (1, 1): [14], (1, 2): [15], (1, 3): [16, 17]}
        STEP_AFTER = {(1, 6): 0, (1, 8): 1, (1, 10): 2, (1, 12): 3}

        def start_ffn(step, prep):
            def after(late, slot):
                for n in PREP_AFTER.get((late, slot), []):
                    prep(NT, 0, n)
                if (late, slot) in STEP_AFTER:
                    step(NT, STEP_AFTER[late, slot], 0, True, False)
            return after

        def attention(piece, per=0, links=None, after=nothing):
            def step(b, p, scores=True, late=True, tail=True, ahead=True):
                for slot in range(SLOTS):
                    piece(b, p, slot, scores, late, tail, ahead)
                    if isinstance(b, int) and b >= BATCH:
                        after(b - BATCH, slot)

            for slot in range(FIRST_LEFT, SLOTS):
                piece(-1, 1, slot, False, False, False, True)
            step(0, 0, late=False, tail=False)
            step(1, 1, tail=False)
            loops = (BATCH - 4) // 2
            with (links[0].engine if links else engine_of[0]).Fori(0, loops) as i:
                if links:
                    for li in links:
                        li.enter(i, per)
                step(2 + 2 * i, 0)
                step(3 + 2 * i, 1)
            if links:
                for li in links:
                    li.leave(loops)
            step(BATCH - 2, 0)
            step(BATCH - 1, 1, ahead=False)
            step(BATCH, 0, scores=False, ahead=False)
            step(BATCH + 1, 1, scores=False, late=False, ahead=False)

        def normed_at(b, slot, first, usual, ahead):
            if isinstance(b, int) and b == -1 and slot == first:
                return True
            return ahead and slot == usual and not (isinstance(b, int) and b == BATCH - 2)

        COMBOS = [(0, 0, True), (1, 0, False), (1, 1, True)]
        S_UNITS = [(half, rep, c) for half in range(2) for rep in range(REP) for c in range(3)]

        S_SLOT = {slot: n for n, slot in enumerate(x for x in range(SLOTS) if x not in (8, 16, 18, 22))}

        @block.sync
        def _(sp):
            sp.dma_start(x_sb[:, 0:SUB, :], x_tok[:, 0:SUB, :]).then_inc(x_loaded, 16)
            for n, group in enumerate(GROUPS):
                e, k = group[0], len(group)
                gates, ups = (ws_gate, ws_up) if e == E else (w_gate[e:e + k], w_up[e:e + k])
                for j, part in enumerate((gates, ups)):
                    src = part if e == E else part.rearrange("e p h -> p e h")
                    dst = w_raw[:, e, j, :] if e == E else w_raw[:, e:e + k, j, :]
                    sp.dma_start(dst, src).then_inc(w_loaded[n], 16)
                for e in group:
                    down = ws_down if e == E else w_down[e]
                    sp.dma_start(w_raw[:, e, 2, :].rearrange("p (c h) -> p c h", c=2),
                                 down.rearrange("(c p) h -> p c h", p=P)).then_inc(w_loaded[n], 16)
            with sp.Fori(1, NT) as t:
                wait_apart(sp, x_loaded, t * 16, passed)
                sp.dma_start(x_sb[:, bass.ds(t * SUB, SUB), :], x_tok[:, bass.ds(t * SUB, SUB), :]).then_inc(x_loaded, 16)
            with sp.Fori(0, NT) as t:
                sp.wait_ge(xnew_done, t + NT + 1)
                sp.dma_start(out_tok[:, bass.ds(t * SUB, SUB), :], x_sb[:, bass.ds(t * SUB, SUB), :]).then_inc(x_stored, 16)
            sp.wait_ge(x_stored, 16 * NT)

        @block.gpsimd
        def _(pool):
            self_ = Links(pool, pool_self)
            g = nc.gpsimd
            pool.dma_start(gw_raw[:], gate_w).then_inc(gw_loaded, 16)
            g.memset(minus_half[:], -0.5).then_inc(consts, 1)
            self_.done(g.memset(ident, 0.0))
            g.affine_select(out=ident_r[:], in_=ident, compare_op=ALU.not_equal, fill=1.0, base=0,
                            pattern=[[-1, P]], channel_multiplier=1).then_inc(consts, 1)

            def early(n):
                if n == 5:
                    self_.done(g.memset(before[:], 1.0))
                    self_.done(g.memset(after[:], 1.0))
                    g.affine_select(out=before[:], in_=before[:], compare_op=ALU.is_gt, fill=0.0, base=0,
                                    pattern=[[1, E], [-1, E]], channel_multiplier=0).then_inc(consts, 1)
                    g.affine_select(out=after[:], in_=after[:], compare_op=ALU.is_gt, fill=0.0, base=0,
                                    pattern=[[-1, E], [1, E]], channel_multiplier=0).then_inc(consts, 1)
                    pool.dma_start(wa_raw[:, 0:QKV], wqkv).then_inc(small_loaded, 16)
                    pool.dma_start(wa_raw[:, QKV:], wo).then_inc(small_loaded, 16)
                    pool.dma_start(rot_sb[:], rot.rearrange("(j p) a d -> p j a d", p=P)).then_inc(small_loaded, 16)
                    pool.dma_start(gain_in[:], q_gain.rearrange("(a h) -> a h", a=1).broadcast_to((P, HEADS))).then_inc(small_loaded, 16)
                    pool.dma_start(lam_in[:], lam.rearrange("(a h) -> a h", a=1).broadcast_to((P, HEADS))).then_inc(small_loaded, 16)
                if n == NCH + LEAD - 1:
                    self_.done(g.memset(ident_b[:], 0.0))
                    self_.done(g.memset(mask_b[:], 0.0))
                    g.affine_select(out=ident_b[:], in_=ident_b[:], compare_op=ALU.not_equal, fill=1.0, base=0,
                                    pattern=[[-1, P]], channel_multiplier=1).then_inc(att_consts, 1)
                    g.affine_select(out=mask_b[:], in_=mask_b[:], compare_op=ALU.is_ge, fill=NEG, base=0,
                                    pattern=[[0, KVH], [-1, P]], channel_multiplier=1).then_inc(att_consts, 1)
                    self_.done(g.memset(qs[:].bitcast(F32), 0.0))
                    self_.done(g.memset(ks[:].bitcast(F32), 0.0))
                    self_.done(g.memset(v1[:], 0.0))
                    g.memset(ks[:, :, :, :, 12:14].bitcast(F32), 1.0)
                    g.memset(v1[:, :, :, :, :, HALF:HALF + 1], 1.0)
                    g.memset(eps_col[:], RMS_EPS)
                    g.memset(kb[:].bitcast(F32), 0.0).then_inc(att_consts, 1)
                    pool.wait_ge(small_loaded, 16 * N_SMALL)
                    g.tensor_copy(cc[:, :, 0:HALF], rot_sb[:, :, 0, :])
                    g.tensor_copy(cc[:, :, HALF:HD], rot_sb[:, :, 0, :])
                    g.tensor_copy(ss[:, :, 0:HALF], rot_sb[:, :, 1, :])
                    g.tensor_scalar(ss[:, :, HALF:HD], rot_sb[:, :, 1, :], -1.0, None, ALU.mult)
                    self_.done(g.memset(gain[:], 1.0))
                    for j in range(2):
                        ins = g.tensor_copy(gain[:, j, 0:HEADS], gain_in[:])
                    ins.then_inc(att_consts, 1)
                    for rep in range(REP):
                        for j in range(2):
                            ins = g.tensor_copy(lam_x[:, rep, j, :, :],
                                                lam_in[:].rearrange("p (r i) -> p r i", i=REP)[:, :, rep:rep + 1]
                                                .broadcast_to((P, KVH, HALF)))
                    ins.then_inc(att_consts, 1)

            def power(t):
                wait_apart(pool, stats_done, t + 1, passed)
                self_.done(g.tensor_scalar(rstd[:], mv[:, :, 1], LN_EPS, 1.0, ALU.add, ALU.mult))
                g.tensor_tensor(rstd[:], rstd[:], minus_half[:, 0:SUB], ALU.pow).then_inc(rstd_done, 1)

            def scale(t, par, k):
                pool.wait_ge(wtok_done, t + 1)
                wait_apart(pool, xwT_done, t * E + k - 2, passed)
                for j in range(SUB):
                    ins = g.tensor_scalar(xw[:, k % 2, j, :], xn[:, par, j, :], w_tok[:, par, j, k - 1:k], 1.0,
                                          ALU.mult, ALU.mult)
                ins.then_inc(xw_done, 1)

            def scale_first(t, par, k):
                wait_apart(pool, wtok_done, t + 1, passed)
                for j in range(SUB):
                    ins = g.tensor_scalar(xw[:, k % 2, j, :], xn[:, par, j, :], w_tok[:, par, j, k - 1:k], 1.0,
                                          ALU.mult, ALU.mult)
                ins.then_inc(xw_done, 1)

            def step(t, n, par, first, last):
                if n % 2 == 0 and 3 <= n // 2 + 2 <= E:
                    scale(t, par, n // 2 + 2)

            def beats(t):
                flat = lambda a: a[:].rearrange("p j e f -> p j (e f)")
                over = lambda a: a[:].rearrange("p (o e) f -> p o (e f)", o=1).broadcast_to((P, SUB, E * E))
                wait_apart(pool, cmp_done, t + 1, passed)
                g.tensor_tensor(flat(cmp_ge), flat(cmp_ge), over(before), ALU.mult)
                self_.done(g.tensor_tensor(flat(cmp_gt), flat(cmp_gt), over(after), ALU.mult))
                g.tensor_tensor(flat(cmp_ge), flat(cmp_ge), flat(cmp_gt), ALU.add).then_inc(beats_done, 1)

            def prep_at(stage):
                def prep(t, par, n):
                    if n == 4:
                        power(t)
                    if n == 11:
                        beats(t)
                    if n == 17:
                        for k in (1, 2):
                            (scale_first if isinstance(t, int) and t == 0 else scale)(t, par, k)
                return prep

            def piece(b, p, slot, scores, late, tail, ahead):
                if isinstance(b, int) and b == -1 and slot == 0:
                    pool.wait_ge(att_consts, N_ATT)
                if normed_at(b, slot, 2, 24, ahead):
                    wait_apart(pool, a_stats, b + 2 + (slot == 24), passed)
                    self_.done(g.tensor_scalar(arstd[:], amv[:, :, 1], LN_EPS, 1.0, ALU.add, ALU.mult))
                    g.tensor_tensor(arstd[:], arstd[:], minus_half[:, 0:2], ALU.pow).then_inc(a_rstd, 1)
                if scores and slot == 5:
                    gated_values(b, p)
                if ahead and slot == 17:
                    if not (isinstance(b, int) and b < 1):
                        wait_apart(pool, q2T_done, b * 4, passed)
                    g.memset(qs[:, 1 - p].rearrange("p j h i r c -> p (j h i r) c")[:, :, 12:14].bitcast(F32),
                             0.0).then_inc(a_clear, 1)
                if ahead and slot == 11:
                    wait_apart(pool, a_r0, b + 2, passed)
                    self_.done(g.tensor_scalar(ma[:], ms[:], 1.0 / HD, RMS_EPS, ALU.mult, ALU.add))
                    self_.done(g.tensor_tensor(ma[:], ma[:], r0[:], ALU.mult))
                    self_.done(g.tensor_tensor(ma[:], ma[:], r0[:], ALU.mult), apart=passed)
                    self_.done(g.tensor_scalar(ma[:], ma[:], -0.5, 1.5, ALU.mult, ALU.add))
                    self_.done(g.tensor_tensor(ma[:], ma[:], r0[:], ALU.mult))
                    g.tensor_tensor(rq[:], ma[:], gain[:], ALU.mult).then_inc(a_rq, 1)
                u = slot - T_LAG
                if late and u >= 0:
                    hp, j = u // 6, u % 6
                    wait_apart(pool, exp_done, (b - 1) * UNITS + u + 1, passed)
                    if j < 4:
                        v = pr[:, hp % 2, j, :].rearrange("p (i q) -> p i q", i=2)[:, :, 0:P]
                        pat = [[0, 2], [1, P]]
                    else:
                        v = pr[:, hp % 2, j, :].rearrange("p (i q) -> p i q", i=4)
                        pat = [[0, 4], [1, P]]
                    g.affine_select(out=v, in_=v, compare_op=ALU.is_ge, fill=0.0, base=0,
                                    pattern=pat, channel_multiplier=-1).then_inc(sel_done, 1)

            def gated_values(b, p):
                pool.wait_ge(a_sig, b + 1)
                if not (isinstance(b, int) and b < 2):
                    pool.wait_ge(pv_done, (b - 1) * 4)
                for j in range(2):
                    vv = qkv[:, j, NH * HD:NH * HD + KVH * HD].rearrange("p (r d) -> p r d", r=KVH)
                    gg = eg[:, j, :].rearrange("p (r d) -> p r d", r=KVH)
                    for half in range(2):
                        d = slice(HALF * half, HALF * half + HALF)
                        ins = g.tensor_tensor(v1[:, p, j, half, :, 0:HALF], vv[:, :, d], gg[:, :, d], ALU.mult)
                ins.then_inc(a_v, 1)

            engine_of[0] = pool
            ffn_stage(0, step, prep_at(0), nothing, nothing, [self_], 4, early, meanwhile=start_attention(piece))
            attention(piece, 2 * 6, [self_], start_ffn(step, prep_at(1)))
            ffn_stage(1, step, prep_at(1), nothing, nothing, [self_], 4, begun=True)

        @block.scalar
        def _(act):
            s = nc.scalar
            self_ = Links(act, act_self)
            engine_of[0] = act
            def expert_hi(m):
                n = [ORDER[m] in group for group in GROUPS].index(True)
                act.wait_ge(w_loaded[n], 16 * (2 + len(GROUPS[n])))
                s.copy(w_hi[:, ORDER[m]], w_raw[:, ORDER[m]]).then_inc(w_hi_done, 1)

            def early(n):
                if n == 5:
                    act.wait_ge(gw_loaded, 16)
                    s.copy(gw_hi, gw_raw[:]).then_inc(w_hi_done, 1)
                if n in SPLIT_AT:
                    for m in SPLIT_AT[n]:
                        expert_hi(m)
                if n == NCH + LEAD - 1:
                    act.wait_ge(small_loaded, 16 * N_SMALL)
                    s.copy(wa_hi[:], wa_raw[:]).then_inc(w_hi_done, 1)

            def step(t, n, par, first, last):
                c = t * NCH + n
                act.wait_ge(g_done, c + 1)
                if isinstance(t, int) and t == NT and n == 0:
                    act.wait_ge(oT_done, 4 * BATCH)
                if not (isinstance(t, int) and t == 0 and n < 2):
                    act.wait_ge(hid_done, c - 1)
                s.activation(act_g[:, n % 2, :], g_ps[n % 2][:], ACT.Silu).then_inc(silu_done, 1)
                if not (first and n == 0):
                    top(t, n - 1)
                if n % 2 == 0 and n // 2 + 1 <= E:
                    k = n // 2 + 1
                    act.wait_ge(xwT_done, t * E + k)
                    if not (isinstance(t, int) and t == 0 and k < 3):
                        act.wait_ge(u_done, c - 2 if k > 2 else c - 1)
                    s.copy(xw_hi[:, k % 2, :], xw_ps[:]).then_inc(xwhi_done, 1)
                if n == 1 and not first:
                    output(t - 1)

            def top(t, n):
                m = t * NCH + n
                act.wait_ge(hid_done, m + 1)
                if not (isinstance(t, int) and t == 0 and n < 3):
                    act.wait_ge(down_done, m - 2)
                s.copy(h_hi[:, n % 3, :], hid[:, n % 2, :]).then_inc(hhi_done, 1)

            def output(t):
                act.wait_ge(down_done, (t + 1) * NCH)
                s.activation(y_sb[:], y_ps[:], ACT.Copy, scale=0.5).then_inc(y_done, 1)

            def prep(t, par, n):
                if n == 7:
                    act.wait_ge(xnT_done, t + 1)
                    if isinstance(t, int) and t == NT:
                        act.wait_ge(s_done, BATCH * UNITS)
                    s.copy(x_hi[:, par, :], prep_ps[:]).then_inc(xhi_done, 1)
                if n == 10:
                    act.wait_ge(lsub_done, t + 1)
                    s.activation(th[:], lsub[:], ACT.Tanh, scale=0.5).then_inc(tanh_done, 1)

            def tail(t, par):
                top(t, NCH - 1)
                output(t)

            def piece(b, p, slot, scores, late, tail, ahead):
                if isinstance(b, int) and b == -1 and slot == 0:
                    act.wait_ge(att_consts, N_ATT)
                if late and slot in (3, 8, 12, 18):
                    hp = (3, 8, 12, 18).index(slot)
                    act.wait_ge(q2T_done, (b - 1) * 4 + hp + 1)
                    s.copy(q2[:, hp // 2, 2 * (hp % 2):2 * (hp % 2) + 2, :],
                           qT_ps[:].rearrange("p (i q) -> p i q", i=2)).then_inc(q2_done, 1)
                if ahead and slot == 5:
                    act.wait_ge(a_xnT, b + 2)
                    s.copy(xa_hi[:], a_ps[:, 0:2 * P]).then_inc(a_xhi, 1)
                if isinstance(b, int) and b == -1 and slot == 8:
                    act.preload_act_table_set("natural_log_exp_and_others")
                if ahead and slot == 8:
                    act.wait_ge(a_proj, b + 2)
                    if not (isinstance(b, int) and b == -1):
                        act.wait_ge(a_stack, 2 * b + 2)
                        act.wait_ge(a_v, b + 1)
                    pj = a_ps[:, 0:2 * QKV].rearrange("p (j c) -> p j c", j=2)
                    s.activation(sq[:].rearrange("p j h d -> p j (h d)"), pj[:, :, 0:NH * HD], ACT.Square)
                    s.copy(qkv[:], pj).then_inc(a_qkv, 1)
                    s.activation(eg[:], pj[:, :, QKV - KVH * HD:QKV], ACT.Exp, scale=-1.0).then_inc(a_eg, 1)
                if ahead and slot == 10:
                    act.wait_ge(a_ms, b + 2)
                    self_.done(s.activation(lnm[:], ms[:], ACT.Ln, bias=eps_col[:], scale=1.0 / HD))
                    s.activation(r0[:], lnm[:], ACT.Exp, scale=-0.5).then_inc(a_r0, 1)
                if ahead and slot == 22:
                    place_keys(b + 1, 1 - p, 0)
                if scores and slot == 0:
                    place_keys(b, p, 1)
                if ahead and slot in (23, 26):
                    place_queries(b + 1, 1 - p, (slot - 23) // 3)
                if scores and slot in (6, 10):
                    place_queries(b, p, 2 + (slot - 6) // 4)
                u = slot - T_LAG
                if late and u >= 0:
                    hp = u // 6
                    act.wait_ge(t_done, (b - 1) * UNITS + u + 1)
                    if u % 6 == 0 and not (isinstance(b, int) and b == 1 and hp < 2):
                        act.wait_ge(pv_done, (b - 1) * 4 + hp - 1)
                    s.activation(pr[:, hp % 2, u % 6, :], t_ps[u % 2][:], ACT.Exp, scale=float(HALF) ** -0.5)\
                        .then_inc(exp_done, 1)
                if late and slot in (14, 20, 26):
                    outputs((b - 1) * 4 + (slot - 14) // 6, (slot - 14) // 6, isinstance(b, int) and b == 1)
                if tail and slot == 4:
                    outputs((b - 2) * 4 + 3, 3, False)
                if tail and slot == 11:
                    act.wait_ge(yaT_done, b - 1)
                    s.copy(ya_hi[:], e_ps[:, 0:2 * P]).then_inc(yahi_done, 1)

            def place_queries(b, p, hp):
                act.wait_ge(a_q1T, b * 4 + hp + 1)
                s.copy(q1[:, p, hp // 2, 2 * (hp % 2):2 * (hp % 2) + 2, :],
                       qT_ps[:].rearrange("p (i q) -> p i q", i=2)).then_inc(a_q1, 1)

            def place_keys(b, p, half):
                act.wait_ge(a_kT, 2 * b + half + 1)
                if not (isinstance(b, int) and b < 2):
                    act.wait_ge(t_done, (b - 2) * UNITS + (half + 1) * UNITS // 2)
                for r in range(KVH):
                    rows = slice(GRP * r, GRP * r + GRP)
                    ins = s.copy(kb[rows, p, half, r, :], a_ps[rows, half * 256:half * 256 + 256])
                ins.then_inc(a_kb, 1)

            def outputs(count, hp, fresh):
                act.wait_ge(pv_done, count + 1)
                if not (fresh and hp < 2):
                    act.wait_ge(oT_done, count - 1)
                s.copy(o_sb[:, hp % 2, :], o_ps[:]).then_inc(o_done, 1)

            ffn_stage(0, step, prep, nothing, tail, early=early, meanwhile=start_attention(piece))
            act.preload_act_table_set("natural_log_exp_and_others")
            attention(piece, 2, [self_], start_ffn(step, prep))
            ffn_stage(1, step, prep, nothing, tail, begun=True)

        @block.vector
        def _(dve):
            v = nc.vector
            engine_of[0] = dve
            self_ = Links(dve, dve_self)

            def early(n):
                if n == 5:
                    dve.wait_ge(w_hi_done, 1)
                    v.tensor_tensor(gw_lo, gw_raw[:], gw_hi.bitcast(F32), ALU.subtract).then_inc(w_lo_done, 1)
                if n == 9:
                    dve.wait_ge(consts, N_CONST)
                if n in SPLIT_AT:
                    for m in SPLIT_AT[n]:
                        e = ORDER[m]
                        dve.wait_ge(w_hi_done, m + 2)
                        v.tensor_tensor(w_lo[:, e], w_raw[:, e], w_hi[:, e].bitcast(F32), ALU.subtract).then_inc(w_lo_done, 1)
                if n == NCH + LEAD - 1:
                    dve.wait_ge(w_hi_done, E + 3)
                    v.tensor_tensor(wa_lo[:], wa_raw[:], wa_hi[:].bitcast(F32), ALU.subtract).then_inc(w_lo_done, 1)

            def step(t, n, par, first, last):
                c = t * NCH + n
                dve.wait_ge(silu_done, c + 1)
                dve.wait_ge(u_done, c + 1)
                if not (isinstance(t, int) and t == 0 and n < 2):
                    dve.wait_ge(hlo_done, c - 1)
                v.tensor_tensor(hid[:, n % 2, :], act_g[:, n % 2, :], u_ps[n % 2][:], ALU.mult).then_inc(hid_done, 1)
                if not (first and n == 0):
                    rest(t, n - 1)
                if n % 2 == 0 and n // 2 + 1 <= E:
                    k = n // 2 + 1
                    dve.wait_ge(xwhi_done, t * E + k)
                    v.tensor_tensor(xw_lo[:, k % 2, :], xw_ps[:], xw_hi[:, k % 2, :].bitcast(F32),
                                    ALU.subtract).then_inc(xwlo_done, 1)

            def rest(t, n):
                dve.wait_ge(hhi_done, t * NCH + n + 1)
                if isinstance(t, int) and t == NT and n == 0:
                    dve.wait_ge(t_done, BATCH * UNITS)
                v.tensor_tensor(h_lo[:, n % 3, :], hid[:, n % 2, :], h_hi[:, n % 3, :].bitcast(F32),
                                ALU.subtract).then_inc(hlo_done, 1)

            def prep_at(stage):
                def prep(t, par, n):
                    tl = t - stage * NT
                    if n == 4:
                        if stage == 0:
                            dve.wait_ge(x_loaded, tl * 16 + 16)
                        elif isinstance(t, int) and t == NT:
                            dve.wait_ge(att_done, TILE // SEQ)
                        for j in range(SUB):
                            ins = v.bn_stats(st[:, j, :], x_sb[:, bass.ds(tl * SUB + j, 1), :].rearrange("p a d -> p (a d)"))
                        self_.done(ins, apart=passed)
                        for j in range(SUB):
                            ins = v.bn_aggr(mv[:, j, :], st[:, j, :])
                        ins.then_inc(stats_done, 1)
                    if n == 5:
                        dve.wait_ge(rstd_done, t + 1)
                        for j in range(SUB):
                            ins = v.tensor_scalar(xn[:, par, j, :],
                                                  x_sb[:, bass.ds(tl * SUB + j, 1), :].rearrange("p a d -> p (a d)"),
                                                  mv[:, j, 0:1], rstd[:, j:j + 1], ALU.subtract, ALU.mult)
                        ins.then_inc(xn_done, 1)
                    if n == 7:
                        dve.wait_ge(xhi_done, t + 1)
                        v.tensor_tensor(x_lo[:, par, :], prep_ps[:], x_hi[:, par, :].bitcast(F32),
                                        ALU.subtract).then_inc(xlo_done, 1)
                    if n == 9:
                        dve.wait_ge(logits_done, t + 1)
                        lg = fin_ps[:, 0:SUB * 2 * E].rearrange("p (j e) -> p j e", j=SUB)
                        self_.done(v.tensor_copy(prob[:], lg[:, :, E:2 * E]))
                        self_.done(v.tensor_tensor(prob[:], prob[:], lg[:, :, 0:E], ALU.add))
                        self_.done(v.tensor_reduce(lmax[:], prob[:], AX.X, ALU.max))
                        v.tensor_tensor(lsub[:], prob[:], lmax[:].rearrange("p (j a) -> p j a", a=1).broadcast_to((P, SUB, E)),
                                        ALU.subtract).then_inc(lsub_done, 1)
                    if 10 <= n <= 16:
                        gate(t, par, n - 10)
                return prep

            def gate(t, par, part):
                pj = [lsub[:, j:j + 1, :].broadcast_to((P, E, E)) for j in range(SUB)]
                pe_ = [lsub[:, j, :].rearrange("p (e a) -> p e a", a=1).broadcast_to((P, E, E)) for j in range(SUB)]
                if part == 0:
                    dve.wait_ge(lsub_done, t + 1)
                    for j in range(SUB):
                        v.tensor_tensor(cmp_ge[:, j], pj[j], pe_[j], ALU.is_ge)
                if part == 1:
                    for j in range(SUB):
                        ins = v.tensor_tensor(cmp_gt[:, j], pj[j], pe_[j], ALU.is_gt)
                    ins.then_inc(cmp_done, 1)
                if part == 3:
                    dve.wait_ge(beats_done, t + 1)
                    v.tensor_reduce(rank[:], cmp_ge[:], AX.X, ALU.add)
                if part == 4:
                    dve.wait_ge(tanh_done, t + 1)
                    self_.done(v.tensor_scalar(th1[:], th[:], -1.0, 1.0, ALU.mult, ALU.add))
                    self_.done(v.reciprocal(th1[:], th1[:]))
                    self_.done(v.scalar_tensor_tensor(out=prob[:], in0=th[:], scalar=1.0, in1=th1[:],
                                                      op0=ALU.add, op1=ALU.mult))
                if part == 5:
                    if not (isinstance(t, int) and t == 0):
                        dve.wait_ge(wtok_done, t)
                    v.tensor_reduce(total[:], prob[:], AX.X, ALU.add)
                    self_.done(v.scalar_tensor_tensor(out=chosen[:], in0=rank[:], scalar=2.0, in1=prob[:],
                                                      op0=ALU.is_lt, op1=ALU.mult))
                    self_.done(v.tensor_reduce(top2[:], chosen[:], AX.X, ALU.add))
                if part == 6:
                    self_.done(v.scalar_tensor_tensor(out=top2[:], in0=total[:], scalar=1e-20, in1=top2[:],
                                                      op0=ALU.mult, op1=ALU.add))
                    self_.done(v.reciprocal(rtop[:], top2[:]))
                    v.tensor_tensor(w_tok[:, par], chosen[:],
                                    rtop[:].rearrange("p (j a) -> p j a", a=1).broadcast_to((P, SUB, E)),
                                    ALU.mult).then_inc(wtok_done, 1)

            def finish_at(stage):
                def finish(t, par, last):
                    tl = t - stage * NT
                    dve.wait_ge(yT_done, t + 1)
                    xs = x_sb[:, bass.ds(tl * SUB, SUB), :].rearrange("p j d -> p (j d)")
                    v.tensor_tensor(xs, xs, fin_ps[:], ALU.add).then_inc(xnew_done, 1)
                return finish

            def tail(t, par):
                rest(t, NCH - 1)

            def piece(b, p, slot, scores, late, tail, ahead):
                if isinstance(b, int) and b == -1 and slot == 0:
                    dve.wait_ge(att_consts, N_ATT)
                if ahead:
                    project(b + 1, 1 - p, slot)
                if normed_at(b, slot, 1, 23, ahead):
                    statistics(b + 1 + (slot == 23))
                if normed_at(b, slot, 3, 26, ahead):
                    norm(b + 1 + (slot == 26))
                if scores and slot == 4:
                    sigmoid(b)
                if scores and slot == 0 and not (isinstance(b, int) and b < 2):
                    dve.wait_ge(m_done, b - 1)
                if scores and slot in S_SLOT:
                    n = S_SLOT[slot]
                    half, rep, c = S_UNITS[n]
                    dve.wait_ge(s_done, b * UNITS + n + 1)
                    v.tensor_reduce(mx[:, p, c, half, rep, :], s_ps[n % 2][:].rearrange("p (r k) -> p r k", r=KVH),
                                    AX.X, ALU.max).then_inc(max_done, 1)
                if late and slot == 0:
                    maxima(b - 1, 1 - p)
                if late and slot in (17, 23):
                    normalise((b - 1) * 4 + (slot - 17) // 6, (slot - 17) // 6)
                if tail and slot == 1:
                    normalise((b - 2) * 4 + 2, 2)
                if tail and slot == 7:
                    normalise((b - 2) * 4 + 3, 3)
                if tail and slot == 8:
                    combine(b - 2)
                if tail and slot == 12:
                    dve.wait_ge(yahi_done, b - 1)
                    v.tensor_tensor(ya_lo[:], e_ps[:, 0:2 * P], ya_hi[:].bitcast(F32), ALU.subtract).then_inc(yalo_done, 1)
                if tail and slot == 14:
                    dve.wait_ge(wo_done, b - 1)
                    xs = x_sb[:, bass.ds((b - 2) * 2, 2), :].rearrange("p j d -> p (j d)")
                    v.tensor_tensor(xs, xs, e_ps[:, 2 * P:4 * P], ALU.add).then_inc(att_done, 1)

            def sigmoid(b):
                dve.wait_ge(a_eg, b + 1)
                self_.done(v.tensor_scalar(eg[:], eg[:], 1.0, None, ALU.add))
                v.reciprocal(eg[:], eg[:]).then_inc(a_sig, 1)

            def maxima(b, p):
                dve.wait_ge(max_done, (b + 1) * UNITS)
                flat = mx[:, p].rearrange("p c h i r -> p c (h i r)")
                self_.done(v.tensor_tensor(flat[:, 1, :], flat[:, 1, :], flat[:, 2, :], ALU.max))
                m = flat[:, 0:2, :].rearrange("p c g -> p (c g)")
                st_ = qs[:, p].rearrange("p j h i r c -> p (j h i r) c")
                self_.done(v.tensor_scalar(st_[:, :, 12], m, -1.0, None, ALU.mult))
                v.scalar_tensor_tensor(out=st_[:, :, 13], in0=m, scalar=-1.0, in1=st_[:, :, 12].bitcast(F32),
                                       op0=ALU.mult, op1=ALU.subtract).then_inc(m_done, 1)

            def statistics(b):
                for j in range(2):
                    ins = v.bn_stats(ast[:, j, :], x_sb[:, bass.ds(b * 2 + j, 1), :].rearrange("p a d -> p (a d)"))
                self_.done(ins, apart=passed)
                for j in range(2):
                    ins = v.bn_aggr(amv[:, j, :], ast[:, j, :])
                ins.then_inc(a_stats, 1)

            def norm(b):
                dve.wait_ge(a_rstd, b + 1)
                if not (isinstance(b, int) and b == 0):
                    dve.wait_ge(a_xnT, b)
                for j in range(2):
                    ins = v.tensor_scalar(xa[:, j, :], x_sb[:, bass.ds(b * 2 + j, 1), :].rearrange("p a d -> p (a d)"),
                                          amv[:, j, 0:1], arstd[:, j:j + 1], ALU.subtract, ALU.mult)
                ins.then_inc(a_xn, 1)

            def project(b, p, slot):
                if slot == 6:
                    dve.wait_ge(a_xhi, b + 1)
                    v.tensor_tensor(xa_lo[:], a_ps[:, 0:2 * P], xa_hi[:].bitcast(F32), ALU.subtract).then_inc(a_xlo, 1)
                qk = qkv[:, :, 0:NH * HD].rearrange("p j (h d) -> p j h d", h=NH)
                if slot == 9:
                    dve.wait_ge(a_qkv, b + 1)
                    v.tensor_reduce(ms[:], sq[:], AX.X, ALU.add).then_inc(a_ms, 1)
                if slot == 14:
                    dve.wait_ge(a_rq, b + 1)
                    if not (isinstance(b, int) and b == 0):
                        dve.wait_ge(a_stack, 2 * b)
                    for j in range(2):
                        ins = v.tensor_tensor(qn[:, j], qk[:, j],
                                              rq[:, j, :].rearrange("p (h a) -> p h a", a=1).broadcast_to((P, NH, HD)),
                                              ALU.mult)
                    self_.done(ins)
                if slot in (15, 16):
                    j = slot - 15
                    one = lambda a, n: a.rearrange("p (a d) -> p a d", a=1).broadcast_to((P, NH, n))
                    v.tensor_tensor(ra[:, j], qn[:, j], one(cc[:, j, :], HD), ALU.mult)
                    v.tensor_tensor(rb[:, j, :, 0:HALF], qn[:, j, :, HALF:HD], one(ss[:, j, 0:HALF], HALF), ALU.mult)
                    ins = v.tensor_tensor(rb[:, j, :, HALF:HD], qn[:, j, :, 0:HALF], one(ss[:, j, HALF:HD], HALF), ALU.mult)
                    if j == 1:
                        self_.done(ins)
                if slot == 17:
                    self_.done(v.tensor_tensor(ra[:].rearrange("p j h d -> p (j h d)"), ra[:].rearrange("p j h d -> p (j h d)"),
                                               rb[:].rearrange("p j h d -> p (j h d)"), ALU.add))
                if slot in (18, 20, 22, 24):
                    half, j = divmod((slot - 18) // 2, 2)
                    if slot == 18:
                        if not (isinstance(b, int) and b == 0):
                            dve.wait_ge(a_kT, 2 * b)
                        if not (isinstance(b, int) and b < 2):
                            dve.wait_ge(q2T_done, (b - 1) * 4)
                    d = slice(HALF * half, HALF * half + HALF)
                    rq_ = ra[:, j, 0:HEADS].rearrange("p (r i) d -> p i r d", i=REP)[:, :, :, d]
                    rk_ = ra[:, j, HEADS:NH][:, :, d]
                    qs_, ks_ = qs[:, p, j, half], ks[:, j, half]
                    v.tensor_copy(qs_[:, :, :, 0:4], rq_)
                    v.tensor_copy(qs_[:, :, :, 4:8], rq_)
                    v.tensor_copy(ks_[:, :, 0:4], rk_)
                    self_.done(v.tensor_copy(ks_[:, :, 8:12], rk_))
                    v.tensor_tensor(qs_[:, :, :, 8:12], rq_, qs_[:, :, :, 0:4].bitcast(F32), ALU.subtract)
                    ins = v.tensor_tensor(ks_[:, :, 4:8], rk_, ks_[:, :, 0:4].bitcast(F32), ALU.subtract)
                    if j == 1:
                        ins.then_inc(a_stack, 1)

            def normalise(count, hp):
                dve.wait_ge(oT_done, count + 1)
                o = e_ps[:].rearrange("p (g c) -> p g c", c=GRP)
                self_.done(v.reciprocal(rden[:], o[:, :, HALF]))
                v.tensor_tensor(an[:, hp // 2, hp % 2], o[:, :, 0:HALF],
                                rden[:].rearrange("p (g a) -> p g a", a=1).broadcast_to((P, 16, HALF)),
                                ALU.mult).then_inc(an_done, 1)

            def combine(b):
                dve.wait_ge(an_done, (b + 1) * 4)
                flat = an[:].rearrange("p h i g d -> p h (i g d)")
                self_.done(v.tensor_tensor(lt[:], flat[:, 1, :], lam_x[:].rearrange("p i j r d -> p (i j r d)"), ALU.mult))
                a1 = flat[:, 0, :].rearrange("p (i j r d) -> p j i r d", i=REP, j=2, r=KVH)
                l2 = lt[:].rearrange("p (i j r d) -> p j i r d", i=REP, j=2, r=KVH)
                for j in range(2):
                    yo = ya[:, j].rearrange("p (r i) d -> p i r d", i=REP)
                    v.tensor_tensor(yo[:, :, :, 0:HALF], a1[:, j], l2[:, j], ALU.subtract)
                    ins = v.tensor_tensor(yo[:, :, :, HALF:HD], a1[:, j], l2[:, j], ALU.add)
                ins.then_inc(ya_done, 1)

            ffn_stage(0, step, prep_at(0), finish_at(0), tail, [self_], 2 * DVE_FFN, early, meanwhile=start_attention(piece))
            attention(piece, 2 * DVE_ATT, [self_], start_ffn(step, prep_at(1)))
            dve.wait_ge(att_done, BATCH)
            ffn_stage(1, step, prep_at(1), finish_at(1), tail, [self_], 2 * DVE_FFN, begun=True)

        @block.tensor
        def _(pe):
            t_ = nc.tensor
            engine_of[0] = pe
            pe.wait_ge(consts, N_CONST)

            def product(o, w_h, w_l, m_h, m_l, start=True, stop=True):
                t_.matmul(o, w_h, m_h, start=start, stop=False)
                t_.matmul(o, w_l, m_h, start=False, stop=False)
                return t_.matmul(o, w_h, m_l, start=False, stop=stop)

            def step(t, n, par, first, last):
                c = t * NCH + n
                e, h = ORDER[n // 2], (n % 2) * P
                zero = isinstance(t, int) and t == 0
                if n % 2 == 0:
                    pe.wait_ge(w_lo_done, expert_lo(n // 2))
                if isinstance(t, int) and t == NT and n == 0:
                    pe.wait_ge(max_done, BATCH * UNITS)
                    pe.wait_ge(exp_done, BATCH * UNITS)
                    pe.wait_ge(q2_done, 4 * BATCH)
                if isinstance(t, int) and t == NT and n == 2:
                    pe.wait_ge(o_done, 4 * BATCH)
                if n == 0:
                    pe.wait_ge(xhi_done, t + 1)
                    pe.wait_ge(xlo_done, t + 1)
                if not (zero and n < 2):
                    pe.wait_ge(silu_done, c - 1)
                product(g_ps[n % 2][:], w_hi[:, e, 0, h:h + P], w_lo[:, e, 0, h:h + P],
                        x_hi[:, par, :], x_lo[:, par, :]).then_inc(g_done, 1)
                if not (zero and n < 2):
                    pe.wait_ge(hid_done, c - 1)
                k = n // 2
                if k:
                    pe.wait_ge(xwhi_done, t * E + k)
                    pe.wait_ge(xwlo_done, t * E + k)
                    mh, ml = xw_hi[:, k % 2, :], xw_lo[:, k % 2, :]
                else:
                    mh, ml = x_hi[:, par, :], x_lo[:, par, :]
                product(u_ps[n % 2][:], w_hi[:, e, 1, h:h + P], w_lo[:, e, 1, h:h + P], mh, ml).then_inc(u_done, 1)
                if n % 2 == 0 and n // 2 + 1 <= E:
                    k = n // 2 + 1
                    pe.wait_ge(xw_done, t * E + k)
                    if not (zero and k == 1):
                        pe.wait_ge(xwlo_done, t * E + k - 1)
                    for j in range(SUB):
                        ins = t_.transpose(xw_ps[:, j * P:(j + 1) * P], xw[:, k % 2, j, :], ident)
                    ins.then_inc(xwT_done, 1)
                if n >= 2 or not first:
                    down(t, n - 2) if n >= 2 else down(t - 1, n - 2 + NCH)

            def down(t, n):
                c = t * NCH + n
                e, q = ORDER[n // 2], (n % 2) * P
                pe.wait_ge(hhi_done, c + 1)
                pe.wait_ge(hlo_done, c + 1)
                if n == 0 and not (isinstance(t, int) and t == 0):
                    pe.wait_ge(y_done, t)
                product(y_ps[:], w_hi[:, e, 2, q:q + P], w_lo[:, e, 2, q:q + P], h_hi[:, n % 3, :], h_lo[:, n % 3, :],
                        start=n == 0, stop=n == NCH - 1).then_inc(down_done, 1)

            def prep(t, par, n):
                if n == 6:
                    pe.wait_ge(xn_done, t + 1)
                    if isinstance(t, int) and t == NT:
                        pe.wait_ge(a_kb, 2 * BATCH)
                    for j in range(SUB):
                        ins = t_.transpose(prep_ps[:, j * P:(j + 1) * P], xn[:, par, j, :], ident)
                    ins.then_inc(xnT_done, 1)
                if n == 8:
                    pe.wait_ge(xhi_done, t + 1)
                    pe.wait_ge(xlo_done, t + 1)
                    if isinstance(t, int) and t == 0:
                        pe.wait_ge(w_lo_done, 1)
                    if isinstance(t, int) and t == NT:
                        pe.wait_ge(att_done, BATCH - 1)
                    for j in range(SUB):
                        q = slice(j * P, (j + 1) * P)
                        o = 2 * E * j
                        t_.matmul(fin_ps[:, o:o + 2 * E], x_hi[:, par, q], gw_both[:], start=True, stop=False)
                        ins = t_.matmul(fin_ps[:, o:o + E], x_lo[:, par, q], gw_hi, start=False, stop=True)
                    ins.then_inc(logits_done, 1)

            def tail(t, par):
                down(t, NCH - 2)
                down(t, NCH - 1)

            def finish(t, par, last):
                pe.wait_ge(y_done, t + 1)
                pe.wait_ge(lsub_done, t + 1 if last else t + 2)
                for j in range(SUB):
                    ins = t_.transpose(fin_ps[:, j * P:(j + 1) * P], y_sb[:, j * P:(j + 1) * P], ident)
                ins.then_inc(yT_done, 1)

            def piece(b, p, slot, scores, late, tail, ahead):
                if isinstance(b, int) and b == -1 and slot == 0:
                    pe.wait_ge(att_consts, N_ATT)
                    pe.wait_ge(w_lo_done, expert_lo(E + 1))
                if scores and slot in S_SLOT:
                    n = S_SLOT[slot]
                    half, rep, c = S_UNITS[n]
                    qt, kt, edge = COMBOS[c]
                    pe.wait_ge(a_q1, b * 4 + half * 2 + rep // 2 + 1)
                    pe.wait_ge(a_kb, b * 2 + half + 1)
                    if not (isinstance(b, int) and b == 0 and n < 2):
                        pe.wait_ge(max_done, b * UNITS + n - 1)
                    o = s_ps[n % 2][:].rearrange("p (r k) -> p r k", r=KVH)
                    if edge:
                        t_.matmul(o, ident_b[:], mask_b[:], start=True, stop=False)
                    t_.matmul(o, q1[:, p, half, rep, qt * P:(qt + 1) * P], kb[:, p, half, :, kt * P:(kt + 1) * P],
                              start=not edge, stop=True).then_inc(s_done, 1)
                u = slot - T_LAG
                if late and u >= 0:
                    hp, j = u // 6, u % 6
                    half, i0 = hp // 2, 2 * (hp % 2)
                    if j == 0:
                        pe.wait_ge(q2_done, (b - 1) * 4 + hp + 1)
                    if not (isinstance(b, int) and b == 1 and u < 2):
                        pe.wait_ge(exp_done, (b - 1) * UNITS + u - 1)
                    if j < 4:
                        ins = t_.matmul(t_ps[u % 2][:], kb[:, 1 - p, half, j, 0:P], q2[:, half, i0:i0 + 2, :],
                                        start=True, stop=True)
                    else:
                        for r in (2 * (j - 4), 2 * (j - 4) + 1):
                            ins = t_.matmul(t_ps[u % 2][:, (r % 2) * 256:(r % 2) * 256 + 256],
                                            kb[:, 1 - p, half, r, P:2 * P], q2[:, half, i0:i0 + 2, P:2 * P],
                                            start=True, stop=True)
                    ins.then_inc(t_done, 1)
                if late and slot in (2, 7, 11, 17):
                    hp = (2, 7, 11, 17).index(slot)
                    pe.wait_ge(m_done, b)
                    if hp < 3 and scores:
                        pe.wait_ge(a_q1, b * 4 + 2 + hp)
                    elif hp == 0:
                        pe.wait_ge(a_q1, BATCH * 4)
                    else:
                        pe.wait_ge(q2_done, (b - 1) * 4 + hp)
                    turn_queries(1 - p, hp).then_inc(q2T_done, 1)
                if scores and slot in (5, 9):
                    hp = 2 + (slot - 5) // 4
                    pe.wait_ge(a_stack, 2 * b + 2)
                    if late:
                        pe.wait_ge(q2_done, (b - 1) * 4 + hp - 1)
                    else:
                        pe.wait_ge(a_q1, b * 4 + hp)
                    turn_queries(p, hp).then_inc(a_q1T, 1)
                if ahead:
                    project(b + 1, 1 - p, slot, late)
                if late and slot in (12, 13, 18, 19, 24, 25):
                    values(b - 1, (slot - 12) // 6, slot % 2, 1 - p, isinstance(b, int) and b == 1)
                if late and slot == 16 and isinstance(b, int) and b == BATCH:
                    pe.wait_ge(lsub_done, NT + 1)
                if late and slot in (16, 22):
                    turn_outputs((b - 1) * 4 + (slot - 16) // 6, (slot - 16) // 6, isinstance(b, int) and b == 1, b)
                if tail and slot == 0:
                    turn_outputs((b - 2) * 4 + 2, 2, False, b)
                if tail and slot in (2, 3):
                    values(b - 2, 3, slot % 2, p, False)
                if tail and slot == 6:
                    turn_outputs((b - 2) * 4 + 3, 3, False, b)
                if tail and slot == 10:
                    pe.wait_ge(ya_done, b - 1)
                    pe.wait_ge(an_done, (b - 1) * 4)
                    for j in range(2):
                        ins = t_.transpose(e_ps[:, j * P:(j + 1) * P], ya[:, j].rearrange("p h d -> p (h d)"), ident)
                    ins.then_inc(yaT_done, 1)
                if tail and slot == 13:
                    pe.wait_ge(yahi_done, b - 1)
                    pe.wait_ge(yalo_done, b - 1)
                    for j in range(2):
                        q = slice(j * P, (j + 1) * P)
                        ins = product(e_ps[:, (2 + j) * P:(3 + j) * P], ya_hi[:, q], ya_lo[:, q], wa_hi[:, QKV:], wa_lo[:, QKV:])
                    ins.then_inc(wo_done, 1)

            def turn_queries(p, hp):
                half, i0 = hp // 2, 2 * (hp % 2)
                for i in range(2):
                    for j in range(2):
                        o = (2 * i + j) * P
                        ins = t_.transpose(qT_ps[:, o:o + P].bitcast(F32R), qs[:, p, j, half, i0 + i].rearrange("p r c -> p (r c)"), ident_r[:])
                return ins

            def project(b, p, slot, late):
                if slot == 4:
                    pe.wait_ge(a_xn, b + 1)
                    if not (isinstance(b, int) and b == 0):
                        pe.wait_ge(a_kb, b * 2)
                    for j in range(2):
                        ins = t_.transpose(a_ps[:, j * P:(j + 1) * P], xa[:, j, :], ident)
                    ins.then_inc(a_xnT, 1)
                if slot == 7:
                    pe.wait_ge(a_xhi, b + 1)
                    pe.wait_ge(a_xlo, b + 1)
                    for j in range(2):
                        q = slice(j * P, (j + 1) * P)
                        ins = product(a_ps[:, j * QKV:(j + 1) * QKV], xa_hi[:, q], xa_lo[:, q], wa_hi[:, 0:QKV], wa_lo[:, 0:QKV])
                    ins.then_inc(a_proj, 1)
                if slot in (21, 26):
                    half = (slot - 21) // 5
                    pe.wait_ge(a_stack, 2 * b + half + 1)
                    if half:
                        pe.wait_ge(a_kb, 2 * b + 1)
                    else:
                        pe.wait_ge(a_eg, b + 1)
                    for j in range(2):
                        o = (2 * half + j) * P
                        ins = t_.transpose(a_ps[:, o:o + P].bitcast(F32R), ks[:, j, half].rearrange("p r c -> p (r c)"), ident_r[:])
                    ins.then_inc(a_kT, 1)
                if slot in (22, 25):
                    hp = (slot - 22) // 3
                    pe.wait_ge(a_stack, 2 * b + 1)
                    pe.wait_ge(a_clear, b + 1)
                    if hp == 0 and late:
                        pe.wait_ge(q2_done, (b - 1) * 4)
                    elif not (isinstance(b, int) and b == 0 and hp == 0):
                        pe.wait_ge(a_q1, b * 4 + hp)
                    turn_queries(p, hp).then_inc(a_q1T, 1)

            def values(batch, hp, kt, p, fresh):
                count, half = batch * 4 + hp, hp // 2
                if kt == 0:
                    pe.wait_ge(sel_done, count * 6 + 4)
                    pe.wait_ge(a_v, batch + 1)
                    if not (fresh and hp == 0):
                        pe.wait_ge(o_done, count)
                    for r in range(KVH):
                        t_.matmul(o_ps[GRP * r:GRP * r + GRP, :], v1[:, p, 0, half, r, :], pr[:, hp % 2, r, :],
                                  start=True, stop=False)
                else:
                    pe.wait_ge(sel_done, (count + 1) * 6)
                    for r in range(KVH):
                        ins = t_.matmul(o_ps[GRP * r:GRP * r + GRP, :].rearrange("p (i q) -> p i q", i=2)[:, :, P:2 * P],
                                        v1[:, p, 1, half, r, :],
                                        pr[:, hp % 2, 4 + r // 2, (r % 2) * 256:(r % 2) * 256 + 256].rearrange("p (i q) -> p i q", i=2),
                                        start=False, stop=True)
                    ins.then_inc(pv_done, 1)

            def turn_outputs(count, hp, fresh, b):
                pe.wait_ge(o_done, count + 1)
                if not (fresh and hp == 0):
                    pe.wait_ge(an_done, count)
                if hp == 0 and not fresh and not (isinstance(b, int) and b < 2):
                    pe.wait_ge(att_done, b - 1)
                for i in range(4):
                    ins = t_.transpose(e_ps[:, i * P:(i + 1) * P], o_sb[:, hp % 2, i * P:(i + 1) * P], ident)
                ins.then_inc(oT_done, 1)

            ffn_stage(0, step, prep, finish, tail, meanwhile=start_attention(piece))
            pe.wait_ge(xnew_done, NT)
            pe.wait_ge(xwlo_done, NT * E)
            attention(piece, after=start_ffn(step, prep))
            pe.wait_ge(att_done, BATCH)
            ffn_stage(1, step, prep, finish, tail, begun=True)


DVE_FFN = 11
DVE_ATT = 16



def kernel(**inputs):
    import numpy as np
    import concourse.bacc as bacc
    from concourse.bass_utils import run_bass_kernel_spmd

    g = {k: np.asarray(v) for k, v in inputs.items()}
    angles = np.arange(0, HD, 2, dtype=np.float32) / np.float32(HD) * np.float32(np.pi)
    pos = np.arange(SEQ, dtype=np.float32)
    radius = np.float32(1.0) / (np.float32(1.0) + pos[:, None] * np.float32(0.01))
    ang = (pos[:, None] * angles[None, :]).astype(np.float32)
    rot = np.stack([radius * np.cos(ang.astype(np.float64)).astype(np.float32),
                    radius * np.sin(ang.astype(np.float64)).astype(np.float32)], axis=1).astype(np.float32)
    send = {
        "x": g["L0_attn_x"], "w_gate": g["L0_ffn_w_gate"], "w_up": g["L0_ffn_w_up"], "w_down": g["L0_ffn_w_down"],
        "ws_gate": g["L0_ffn_ws_gate"], "ws_up": g["L0_ffn_ws_up"], "ws_down": g["L0_ffn_ws_down"],
        "gate_w": g["L0_ffn_gate_w"],
        "wqkv": np.concatenate([g["L0_attn_Wq"], g["L0_attn_Wk"], g["L0_attn_Wv"], g["L0_attn_Wg"]], axis=0).T,
        "wo": g["L0_attn_Wo"].T, "q_gain": g["L0_attn_q_gain"], "lam": g["L0_attn_lambda_param"], "rot": rot,
    }
    nc = bacc.Bacc("TRN2", target_bir_lowering=False, num_devices=1)
    arrays, args = {}, []
    for name, a in send.items():
        a = np.ascontiguousarray(a)
        arrays[f"in_{name}_dram"] = a
        args.append(nc.dram_tensor(f"in_{name}_dram", a.shape, mybir.dt.from_np(a.dtype), kind="ExternalInput").ap())
    o = nc.dram_tensor("out_0_dram", (BATCH, SEQ, DIM), F32, kind="ExternalOutput").ap()
    macaron(nc, *args, o)
    r = run_bass_kernel_spmd(nc, [arrays], core_ids=[0])
    return r.results[0]["out_0_dram"]
```
